# Optimizing a Trainium2 kernel written in Bass

```python
import numpy as np
import jax
import jax.numpy as jnp

def _softmax(x, axis=-1):
    return jax.nn.softmax(x, axis=axis)

def _gelu(x):
    return jax.nn.gelu(x, approximate=True)

def _silu(x):
    return jax.nn.silu(x)

def _sigmoid(x):
    return jax.nn.sigmoid(x)

def _layernorm(x, axis=-1, eps=1e-05):
    m = jnp.mean(x, axis=axis, keepdims=True)
    v = jnp.var(x, axis=axis, keepdims=True)
    return (x - m) / jnp.sqrt(v + eps)

def _scatter_add(tgt, idx, src, axis=0):
    return tgt.at[idx].add(src)

def _segment_sum(src, seg, n):
    return jax.ops.segment_sum(src, seg, n)
kernel_name = 'mk_early_fusion_d1_tok_img512_r4_d07010'

def setup_inputs(seed: int=0):
    np.random.seed(seed)
    _w = jnp.asarray

    def _rec_inputs():
        import jax
        import jax.numpy as jnp
        _rk = jax.random.key(seed)
        x = -0.000392918 + 0.999932 * jax.random.normal(jax.random.fold_in(_rk, 1), (32, 1, 128, 128), jnp.float32)
        txt = 0.229487 + 0.681011 * jax.random.normal(jax.random.fold_in(_rk, 2), (32, 128, 128), jnp.float32)
        return (x, txt)
    x, txt = _rec_inputs()

    def _L0_tok_setup():
        import math
        import jax, jax.numpy as jnp
        import numpy as np
        PW = PH = 16
        EMB = 128
        HID = 128
        B, H, W = (64, 128, 128)
        L = H // PW * (W // PH)
        SIGMA_ZERO = 0.1

        def _f_noise(x):
            return jnp.sign(x) * jnp.sqrt(jnp.abs(x))

        def _noisy_linear(x, w, b, sw, sb, eps_in, eps_out):
            ei = _f_noise(eps_in)
            eo = _f_noise(eps_out)
            w_n = w + sw * (eo[:, None] * ei[None, :])
            b_n = b + sb * eo
            return x @ w_n.T + b_n

        def _unfold_patches(x):
            b = x.shape[0]
            p = x.reshape(b, H // PW, PW, W // PH, PH)
            p = p.transpose(0, 1, 3, 2, 4)
            return p.reshape(b, L, PW * PH)

        def _pos_encoding(x):
            pos = jnp.arange(L, dtype=jnp.float32)[:, None]
            div = jnp.exp(jnp.arange(0, EMB, 2, dtype=jnp.float32) * (-math.log(10000.0) / EMB))
            ang = pos * div
            pe = jnp.stack([jnp.sin(ang), jnp.cos(ang)], axis=-1).reshape(L, EMB)
            return x + pe[None, :, :]
        key = jax.random.key(seed)
        ks = jax.random.split(key, 12)
        in_f = PW * PH
        sig = SIGMA_ZERO / math.sqrt(in_f)
        bnd1 = 1.0 / math.sqrt(in_f)
        bnd3 = 1.0 / math.sqrt(HID)
        u = lambda k, shape, bnd: jax.random.uniform(k, shape, jnp.float32, -bnd, bnd)
        return {'inputs': jax.random.normal(ks[0], (B, 1, H, W), jnp.float32), 'W1_w': u(ks[1], (HID, in_f), bnd1), 'W1_b': u(ks[2], (HID,), bnd1), 'W1_sw': jnp.full((HID, in_f), sig, jnp.float32), 'W1_sb': jnp.full((HID,), sig, jnp.float32), 'W2_w': u(ks[3], (HID, in_f), bnd1), 'W2_b': u(ks[4], (HID,), bnd1), 'W2_sw': jnp.full((HID, in_f), sig, jnp.float32), 'W2_sb': jnp.full((HID,), sig, jnp.float32), 'W3_w': u(ks[5], (EMB, HID), bnd3), 'W3_b': u(ks[6], (EMB,), bnd3), 'eps_in1': jax.random.normal(ks[7], (in_f,), jnp.float32), 'eps_out1': jax.random.normal(ks[8], (HID,), jnp.float32), 'eps_in2': jax.random.normal(ks[9], (in_f,), jnp.float32), 'eps_out2': jax.random.normal(ks[10], (HID,), jnp.float32)}
    _L0_tok_all = _L0_tok_setup()
    _L0_tok_in = {k: v for k, v in _L0_tok_all.items() if k in ('W1_w', 'W1_b', 'W1_sw', 'W1_sb', 'W2_w', 'W2_b', 'W2_sw', 'W2_sb', 'W3_w', 'W3_b', 'eps_in1', 'eps_out1', 'eps_in2', 'eps_out2')}
    del _L0_tok_all

    def _L0_attn_setup():
        import jax, jax.numpy as jnp
        import numpy as np
        EPS = 1e-05
        key = jax.random.key(seed)
        ks = jax.random.split(key, 6)
        B, T, D, H = (2, 1024, 128, 8)
        bound = float(np.sqrt(6.0 / (D + D)))

        def xavier(k):
            return jax.random.uniform(k, (D, D), jnp.float32, -bound, bound)
        return {'x': jax.random.normal(ks[0], (B, T, D), jnp.float32), 'W_q': xavier(ks[1]), 'W_k': xavier(ks[2]), 'W_v': xavier(ks[3]), 'W_o': xavier(ks[4]), 'ln_gamma': jnp.ones((D,), jnp.float32), 'ln_beta': jnp.zeros((D,), jnp.float32)}
    _L0_attn_all = _L0_attn_setup()
    _L0_attn_in = {k: v for k, v in _L0_attn_all.items() if k in ('W_q', 'W_k', 'W_v', 'W_o', 'ln_gamma', 'ln_beta')}
    del _L0_attn_all

    def _L0_ffn_setup():
        import jax, jax.numpy as jnp
        import numpy as np
        K = 2
        EPS = 1e-06

        def _layernorm(x, gamma, beta):
            mu = jnp.mean(x, axis=-1, keepdims=True)
            var = jnp.mean(jnp.square(x - mu), axis=-1, keepdims=True)
            return (x - mu) * jax.lax.rsqrt(var + EPS) * gamma + beta
        key = jax.random.key(seed)
        ks = jax.random.split(key, 5)
        B, S, D, F, E = (8, 512, 128, 512, 8)
        x = jax.random.normal(ks[0], (B, S, D), dtype=jnp.float32)
        router_w = jax.random.normal(ks[1], (D, E), dtype=jnp.float32) * 0.02
        w1 = jax.random.normal(ks[2], (E, D, F), dtype=jnp.float32) * 0.02
        b1 = jnp.zeros((E, F), dtype=jnp.float32)
        w2 = jax.random.normal(ks[3], (E, F, D), dtype=jnp.float32) * 0.02
        b2 = jnp.zeros((E, D), dtype=jnp.float32)
        gamma = jnp.ones((E, D), dtype=jnp.float32)
        beta = jnp.zeros((E, D), dtype=jnp.float32)
        return {'x': x, 'router_w': router_w, 'w1': w1, 'b1': b1, 'w2': w2, 'b2': b2, 'gamma': gamma, 'beta': beta}
    _L0_ffn_all = _L0_ffn_setup()
    _L0_ffn_in = {k: v for k, v in _L0_ffn_all.items() if k in ('router_w', 'w1', 'b1', 'w2', 'b2', 'gamma', 'beta')}
    del _L0_ffn_all
    return {'x': x, 'txt': txt, 'L0_tok_W1_w': _L0_tok_in['W1_w'], 'L0_tok_W1_b': _L0_tok_in['W1_b'], 'L0_tok_W1_sw': _L0_tok_in['W1_sw'], 'L0_tok_W1_sb': _L0_tok_in['W1_sb'], 'L0_tok_W2_w': _L0_tok_in['W2_w'], 'L0_tok_W2_b': _L0_tok_in['W2_b'], 'L0_tok_W2_sw': _L0_tok_in['W2_sw'], 'L0_tok_W2_sb': _L0_tok_in['W2_sb'], 'L0_tok_W3_w': _L0_tok_in['W3_w'], 'L0_tok_W3_b': _L0_tok_in['W3_b'], 'L0_tok_eps_in1': _L0_tok_in['eps_in1'], 'L0_tok_eps_out1': _L0_tok_in['eps_out1'], 'L0_tok_eps_in2': _L0_tok_in['eps_in2'], 'L0_tok_eps_out2': _L0_tok_in['eps_out2'], 'L0_attn_W_q': _L0_attn_in['W_q'], 'L0_attn_W_k': _L0_attn_in['W_k'], 'L0_attn_W_v': _L0_attn_in['W_v'], 'L0_attn_W_o': _L0_attn_in['W_o'], 'L0_attn_ln_gamma': _L0_attn_in['ln_gamma'], 'L0_attn_ln_beta': _L0_attn_in['ln_beta'], 'L0_ffn_router_w': _L0_ffn_in['router_w'], 'L0_ffn_w1': _L0_ffn_in['w1'], 'L0_ffn_b1': _L0_ffn_in['b1'], 'L0_ffn_w2': _L0_ffn_in['w2'], 'L0_ffn_b2': _L0_ffn_in['b2'], 'L0_ffn_gamma': _L0_ffn_in['gamma'], 'L0_ffn_beta': _L0_ffn_in['beta']}

def reference(x, txt, L0_tok_W1_w, L0_tok_W1_b, L0_tok_W1_sw, L0_tok_W1_sb, L0_tok_W2_w, L0_tok_W2_b, L0_tok_W2_sw, L0_tok_W2_sb, L0_tok_W3_w, L0_tok_W3_b, L0_tok_eps_in1, L0_tok_eps_out1, L0_tok_eps_in2, L0_tok_eps_out2, L0_attn_W_q, L0_attn_W_k, L0_attn_W_v, L0_attn_W_o, L0_attn_ln_gamma, L0_attn_ln_beta, L0_ffn_router_w, L0_ffn_w1, L0_ffn_b1, L0_ffn_w2, L0_ffn_b2, L0_ffn_gamma, L0_ffn_beta):
    import jax
    import jax.numpy as jnp

    def _L0_tok_ref(inputs, W1_w, W1_b, W1_sw, W1_sb, W2_w, W2_b, W2_sw, W2_sb, W3_w, W3_b, eps_in1, eps_out1, eps_in2, eps_out2):
        import math
        import jax, jax.numpy as jnp
        import numpy as np
        PW = PH = 16
        EMB = 128
        HID = 128
        B, H, W = (64, 128, 128)
        L = H // PW * (W // PH)
        SIGMA_ZERO = 0.1

        def _f_noise(x):
            return jnp.sign(x) * jnp.sqrt(jnp.abs(x))

        def _noisy_linear(x, w, b, sw, sb, eps_in, eps_out):
            ei = _f_noise(eps_in)
            eo = _f_noise(eps_out)
            w_n = w + sw * (eo[:, None] * ei[None, :])
            b_n = b + sb * eo
            return x @ w_n.T + b_n

        def _unfold_patches(x):
            b = x.shape[0]
            p = x.reshape(b, H // PW, PW, W // PH, PH)
            p = p.transpose(0, 1, 3, 2, 4)
            return p.reshape(b, L, PW * PH)

        def _pos_encoding(x):
            pos = jnp.arange(L, dtype=jnp.float32)[:, None]
            div = jnp.exp(jnp.arange(0, EMB, 2, dtype=jnp.float32) * (-math.log(10000.0) / EMB))
            ang = pos * div
            pe = jnp.stack([jnp.sin(ang), jnp.cos(ang)], axis=-1).reshape(L, EMB)
            return x + pe[None, :, :]
        x = _unfold_patches(inputs)
        g = _noisy_linear(x, W1_w, W1_b, W1_sw, W1_sb, eps_in1, eps_out1)
        x_gate = g * jnp.tanh(jax.nn.softplus(g))
        x_inner = _noisy_linear(x, W2_w, W2_b, W2_sw, W2_sb, eps_in2, eps_out2)
        x = x_gate * x_inner
        x = x @ W3_w.T + W3_b
        return _pos_encoding(x)

    def _L0_attn_ref(x, W_q, W_k, W_v, W_o, ln_gamma, ln_beta):
        import jax, jax.numpy as jnp
        import numpy as np
        EPS = 1e-05
        B, T, D = x.shape
        H = 8
        hd = D // H
        scale = jnp.sqrt(jnp.asarray(hd, x.dtype))

        def proj(W):
            y = jnp.einsum('btd,ed->bte', x, W)
            return y.reshape(B, T, H, hd).transpose(0, 2, 1, 3)
        Q, K, V = (proj(W_q), proj(W_k), proj(W_v))
        scores = jnp.einsum('bhtd,bhsd->bhts', Q, K) / scale
        attn = jax.nn.softmax(scores, axis=-1)
        ctx = jnp.einsum('bhts,bhsd->bhtd', attn, V)
        ctx = ctx.transpose(0, 2, 1, 3).reshape(B, T, D)
        out = jnp.einsum('btd,ed->bte', ctx, W_o)
        y = out + x
        mu = jnp.mean(y, axis=-1, keepdims=True)
        var = jnp.var(y, axis=-1, keepdims=True)
        return (y - mu) * jax.lax.rsqrt(var + EPS) * ln_gamma + ln_beta

    def _L0_ffn_ref(x, router_w, w1, b1, w2, b2, gamma, beta):
        import jax, jax.numpy as jnp
        import numpy as np
        K = 2
        EPS = 1e-06

        def _layernorm(x, gamma, beta):
            mu = jnp.mean(x, axis=-1, keepdims=True)
            var = jnp.mean(jnp.square(x - mu), axis=-1, keepdims=True)
            return (x - mu) * jax.lax.rsqrt(var + EPS) * gamma + beta
        B, S, D = x.shape
        E = w1.shape[0]
        xf = x.reshape(-1, D)
        logits = xf @ router_w
        gate_vals, idx = jax.lax.top_k(logits, K)
        gates = jax.nn.softmax(gate_vals, axis=-1)
        out = jnp.zeros_like(xf)
        for e in range(E):
            h = jax.nn.relu(xf @ w1[e] + b1[e]) @ w2[e] + b2[e]
            y = _layernorm(xf + h, gamma[e], beta[e])
            w = jnp.sum(jnp.where(idx == e, gates, 0.0), axis=-1)
            out = out + w[:, None] * y
        return out.reshape(B, S, D)
    h = _L0_tok_ref(x, L0_tok_W1_w, L0_tok_W1_b, L0_tok_W1_sw, L0_tok_W1_sb, L0_tok_W2_w, L0_tok_W2_b, L0_tok_W2_sw, L0_tok_W2_sb, L0_tok_W3_w, L0_tok_W3_b, L0_tok_eps_in1, L0_tok_eps_out1, L0_tok_eps_in2, L0_tok_eps_out2)
    h = jnp.concatenate([h, txt], axis=1)
    h = h + _L0_attn_ref(_layernorm(h, axis=-1), L0_attn_W_q, L0_attn_W_k, L0_attn_W_v, L0_attn_W_o, L0_attn_ln_gamma, L0_attn_ln_beta)
    h = h + _L0_ffn_ref(_layernorm(h, axis=-1), L0_ffn_router_w, L0_ffn_w1, L0_ffn_b1, L0_ffn_w2, L0_ffn_b2, L0_ffn_gamma, L0_ffn_beta)
    return h

_drawn_inputs = setup_inputs


def setup_inputs(seed=0):
    import zlib

    import numpy as np

    out = dict(_drawn_inputs(seed))
    spreads = {'L0_tok_W1_sw': (0.0062500000931322575, 0.6),
     'L0_tok_W1_sb': (0.0062500000931322575, 0.6),
     'L0_tok_W2_sw': (0.0062500000931322575, 0.6),
     'L0_tok_W2_sb': (0.0062500000931322575, 0.6),
     'L0_attn_ln_gamma': (1.0, 0.2),
     'L0_attn_ln_beta': (0.0, 0.1),
     'L0_ffn_b1': (0.0, 0.8),
     'L0_ffn_b2': (0.0, 0.304),
     'L0_ffn_gamma': (1.0, 0.2),
     'L0_ffn_beta': (0.0, 0.309)}
    factors = {'L0_tok_W1_b': 6.683,
     'L0_tok_W2_b': 6.55,
     'L0_tok_eps_in1': 3.172,
     'L0_tok_eps_out1': 3.036,
     'L0_tok_eps_in2': 3.007,
     'L0_tok_eps_out2': 2.852,
     'L0_ffn_w1': 3.428,
     'L0_ffn_w2': 2.727}
    for name, (base, spread) in spreads.items():
        noise = np.random.default_rng([zlib.crc32(name.encode()), seed]).standard_normal(out[name].shape)
        drawn = base * np.exp(spread * noise) if base else spread * noise
        out[name] = jnp.asarray(drawn.astype(out[name].dtype))
    for name, factor in factors.items():
        out[name] = (out[name] * factor).astype(out[name].dtype)
    return out
```

```python
from contextlib import ExitStack

import numpy as np

import concourse.bass as bass
from concourse import mybir

ALU = mybir.AluOpType
ACT = mybir.ActivationFunctionType
AX = mybir.AxisListType
F32 = mybir.dt.float32
F16 = mybir.dt.float16
BF16 = mybir.dt.bfloat16
I32 = mybir.dt.int32
U32 = mybir.dt.uint32

P = 128
IMAGES, TXT, D = 32, 128, 128
PAT = 64
SEQ = PAT + TXT
COLS = 2 * SEQ
PAIRS = IMAGES // 2
TILES = COLS // P
TOKENS = IMAGES * SEQ
HEADS, HD = 8, 16
NE, F = 8, 512
FC = F // P
STACK = 49
MAXROW = 64.0
G = 256
GRID = 56
assert GRID >= 2 * TOKENS // G + NE - 1 and GRID % 4 == 0
CAP = TOKENS + G
ROW = 132
H2ROW = D + 2
WROW1, WROW2 = 2 * F, 2 * FC * D + 2 * 2 * D + 2
FAR = 1.0e6
EPS_ATT, EPS_FFN, EPS_LN = 1e-5, 1e-6, 1e-5


class Pair:

    def __init__(self, loop, off, unroll=2):
        self.loop, self.off, self.unroll = loop, off, unroll

    def back(self, n):
        return Pair(self.loop, self.off - n, self.unroll)

    @property
    def exists(self):
        return self.loop is not None or self.off >= 0

    @property
    def number(self):
        return self.off if self.loop is None else self.loop * self.unroll + self.off

    @property
    def par(self):
        return self.off % 2

    @property
    def slot(self):
        return self.off % 4

    def nth_of(self, ring):
        if self.loop is None:
            return self.off // ring
        return self.loop * (self.unroll // ring) + self.off // ring


def wait(eng, sem, per, pair, count, first_wait=None):
    if pair.exists:
        value = pair.number * per + count
        if first_wait and pair.loop is not None:
            eng.compute_val(value)
            first_wait(eng)
        eng.wait_ge(sem, value)


def wait_dma(eng, sems, per, pair, ring=2):
    if pair.exists:
        eng.wait_ge(sems[pair.off % ring], pair.nth_of(ring) * (16 * per) + 16 * per)


class Chain:

    def __init__(self, eng, sem, per, pair):
        self.eng, self.sem, self.per, self.pair, self.n = eng, sem, per, pair, 0

    def __call__(self, ins, first_wait=None):
        self.n += 1
        ins.then_inc(self.sem, 1)
        value = self.pair.number * self.per + self.n
        if first_wait and self.pair.loop is not None:
            self.eng.compute_val(value)
            first_wait(self.eng)
        self.eng.wait_ge(self.sem, value)

    def end(self):
        assert self.n == self.per, (self.n, self.per)


UNITS = 12


def unit(n):
    group, i = divmod(n, 6)
    js = (2 * group, 2 * group + 1) if i in (2, 3) else (2 * group + i // 4,)
    return n % 2, js


def halves(ap2d, width):
    return bass.AP(ap2d.tensor, ap2d.offset, [list(ap2d.ap[0]), [COLS - PAT, 2], [1, width]])


def tile_cols(ap2d, k):
    if k == 0:
        return halves(ap2d, PAT)
    return ap2d[:, PAT + (k - 1) * TXT:PAT + k * TXT]


def early_fusion(nc, a, out):
    ctx = ExitStack()
    with ctx:
        def sb(name, shape, dt=F32):
            return ctx.enter_context(nc.sbuf_tensor(name, shape, dt))

        def sem(name):
            return ctx.enter_context(nc.semaphore(name))

        def sems(name, n=2):
            return [sem(f"{name}{i}") for i in range(n)]

        def dram(name, shape, dt=F32):
            return nc.dram_tensor(name, shape, dt).ap()

        bank = [ctx.enter_context(nc.psum_tensor(f"bank{i}", [P, 512], F32)) for i in range(8)]

        stack_d = dram("stack_d", [2, 4, P, COLS], F16)
        sorted_d = dram("sorted_d", [(NE + 1) * CAP, ROW])
        expert_d = dram("expert_d", [2 * TOKENS, D])
        kept_d = dram("kept_d", [PAIRS, P, TILES * H2ROW])
        w1_d = dram("w1_d", [NE, P, WROW1], F16)
        w2_d = dram("w2_d", [NE, P, WROW2 // 2], I32)
        bias_d = dram("bias_d", [NE, 2, F + D], F16)

        ident = sb("ident", [P, P])
        onesb = sb("onesb", [P, P], BF16)
        before = sb("before", [P, P], BF16)
        iota8 = sb("iota8", [P, NE])
        ecap = sb("ecap", [P, NE])
        iotag = sb("iotag", [P, GRID])
        w12 = sb("w12", [P, 2, 2, P])
        sw12 = sb("sw12", [P, 2, 2, P])
        nrow = sb("nrow", [1, 768])
        nrow2 = sb("nrow2", [1, 2, 768])
        ncol = sb("ncol", [P, 6])
        ncol2 = sb("ncol2", [P, 6])
        w3 = sb("w3", [P, P])
        posb = sb("posb", [P, D])
        b3r = sb("b3r", [P, D])
        wqkv = sb("wqkv", [P, 3, P])
        wo = sb("wo", [P, P])
        lng = sb("lng", [P, D])
        lnb = sb("lnb", [P, D])
        rw = sb("rw", [P, NE])
        stage = [sb(f"stage{i}", [P, 2, F]) for i in range(2)]
        split1 = [sb(f"split1_{i}", [P, WROW1], F16) for i in range(2)]
        split2 = [sb(f"split2_{i}", [P, WROW2], F16) for i in range(2)]
        bstage = sb("bstage", [64, NE * (F + D)])
        bsplit = sb("bsplit", [64, NE * (F + D)], F16)
        padrow = sb("padrow", [P, ROW])
        ones16x = sb("ones16x", [P, G], F16)
        lane = sb("lane", [P, 2])

        xin = [sb(f"xin{i}", [P, 2, P]) for i in range(2)]
        h = [sb(f"h{i}", [P, TILES, D]) for i in range(2)]
        gm = sb("gm", [P, P])
        ge = sb("ge", [P, P])
        gn = sb("gn", [P, P])
        gr = sb("gr", [P, P])
        gt = sb("gt", [P, P])
        gg = sb("gg", [P, P])
        ga = sb("ga", [P, P])
        stat1 = sb("stat1", [P, TILES, 6])
        mv1 = sb("mv1", [P, TILES, 2])
        ve1 = sb("ve1", [P, 2, TILES])
        rs1 = sb("rs1", [P, TILES])
        nm1 = sb("nm1", [P, TILES])
        xn = [sb(f"xn{i}", [P, TILES, D]) for i in range(2)]
        xT = sb("xT", [P, COLS])
        kq = sb("kq", [P, 4, COLS], F16)
        kst = [sb(f"kst{i}", [P, 4, COLS], F16) for i in range(2)]
        qst = [sb(f"qst{i}", [P, 4, COLS], F16) for i in range(2)]
        vx = [sb(f"vx{i}", [P, 4, HEADS, 2 * HD]) for i in range(2)]
        mx = sb("mx", [P, TILES, 2, 4])
        mxT = sb("mxT", [HEADS, COLS], F16)
        pex = [sb(f"pex{i}", [P, COLS]) for i in range(UNITS)]
        cx = [sb(f"cx{i}", [P, COLS]) for i in range(2)]
        rden = sb("rden", [P, TILES, HEADS])
        cn = sb("cn", [P, TILES, D])
        cT = sb("cT", [P, COLS])
        y = sb("y", [P, TILES, D])
        stat2 = sb("stat2", [P, TILES, 6])
        mv2 = sb("mv2", [P, TILES, 2])
        ve2 = sb("ve2", [P, 2, TILES])
        rs2 = sb("rs2", [P, TILES])
        nm2 = sb("nm2", [P, TILES])
        yn = sb("yn", [P, TILES, D])
        yg = sb("yg", [P, TILES, D])
        kept = [sb(f"kept{i}", [P, TILES, H2ROW]) for i in range(2)]
        stat3 = sb("stat3", [P, TILES, 6])
        mv3 = sb("mv3", [P, TILES, 2])
        ve3 = sb("ve3", [P, 2, TILES])
        rs3 = sb("rs3", [P, TILES])
        nm3 = sb("nm3", [P, TILES])
        pay = [sb(f"pay{i}", [P, TILES, ROW]) for i in range(2)]
        x2T = sb("x2T", [P, COLS])
        lg = sb("lg", [P, TILES, NE])
        top = sb("top", [P, TILES, 8])
        topi = sb("topi", [P, TILES, 8], U32)
        topf = sb("topf", [P, TILES, 2])
        gap = sb("gap", [P, TILES])
        gex = sb("gex", [P, TILES])
        gsum = sb("gsum", [P, TILES])
        oh1 = sb("oh1", [P, TILES, NE])
        oh2 = sb("oh2", [P, TILES, NE])
        ohs = sb("ohs", [P, TILES, NE], BF16)
        base = sb("base", [P, NE])
        rank = sb("rank", [P, TILES, NE])
        sl1 = sb("sl1", [P, TILES, NE])
        sl2 = sb("sl2", [P, TILES, NE])
        slf = sb("slf", [P, 2, TILES])
        slot = [sb(f"slot{i}", [P, 2, TILES], U32) for i in range(2)]
        tok = sb("tok", [P, TILES])

        cnt = sb("cnt", [P, NE])
        cnti = sb("cnti", [P, NE], I32)
        cntt = sb("cntt", [P, NE], I32)
        ntl = sb("ntl", [P, NE])
        one8 = sb("one8", [P, NE])
        cum = sb("cum", [P, NE])
        past = sb("past", [P, GRID, NE])
        pastn = sb("pastn", [P, GRID, NE])
        eg = sb("eg", [P, GRID])
        cg = sb("cg", [P, GRID])
        rg = sb("rg", [P, GRID])
        rg2 = sb("rg2", [P, GRID])
        plan = sb("plan", [P, 2, GRID], I32)
        padf = sb("padf", [P, 2, NE])
        padi = sb("padi", [P, 2, NE], U32)

        xs = [sb(f"xs{i}", [P, 2, ROW]) for i in range(4)]
        w1s = [sb(f"w1s{i}", [P, 2, F], F16) for i in range(2)]
        w2s = [sb(f"w2s{i}", [P, WROW2], F16) for i in range(2)]
        bs = [sb(f"bs{i}", [2, F + D], F16) for i in range(4)]
        xsT = [sb(f"xsT{i}", [P, 2, G], F16) for i in range(2)]
        hid = [sb(f"hid{i}", [P, 2, FC, G], F16) for i in range(2)]
        z = sb("z", [P, 2, D])
        stat4 = sb("stat4", [P, 2, 6])
        mv4 = sb("mv4", [P, 2, 2])
        ve4 = sb("ve4", [P, 2, 2])
        neghalf = sb("neghalf", [P, TILES])
        nm4 = [sb(f"nm4_{i}", [P, 2]) for i in range(2)]
        rs4b = [sb(f"rs4b_{i}", [P, 2]) for i in range(2)]
        zn = [sb(f"zn{i}", [P, 2, D]) for i in range(2)]
        zg = sb("zg", [P, 2, D])
        ye = [sb(f"ye{i}", [P, 2, D]) for i in range(2)]
        first = sb("first", [P, 2])
        dest = [sb(f"dest{i}", [P, 2], U32) for i in range(2)]

        y1 = [sb(f"y1_{i}", [P, TILES, D]) for i in range(2)]
        y2 = [sb(f"y2_{i}", [P, TILES, D]) for i in range(2)]
        kc = [sb(f"kc{i}", [P, TILES, H2ROW]) for i in range(2)]
        o1 = [sb(f"o1_{i}", [P, TILES, D]) for i in range(2)]
        o2 = [sb(f"o2_{i}", [P, TILES, D]) for i in range(2)]

        w_in, wa_in = sem("w_in"), sem("wa_in")
        stage_in, split_out = sems("stage_in"), sems("split_out")
        stage_used, split_made = sem("stage_used"), sem("split_made")
        bstage_in, bhi_made, bsplit_made, bsplit_out = sem("bstage_in"), sem("bhi_made"), sem("bsplit_made"), sem("bsplit_out")
        const_made, pool_prep, dve_prep = sem("const_made"), sem("pool_prep"), sem("dve_prep")
        noise_root, noise_row, noise_outer, noise_done = sem("noise_root"), sem("noise_row"), sem("noise_outer"), sem("noise_done")
        xin_in, txt_in = sems("xin_in"), sems("txt_in")
        kq_out, st_in, max_in, kept_out, sent = sems("kq_out"), sems("st_in"), sems("max_in"), sems("kept_out"), sems("sent")
        pe_tok, pe_w3, pe_tr, pe_x2tr, pe_qk, pe_v = [sem(n) for n in ("pe_tok", "pe_w3", "pe_tr", "pe_x2tr", "pe_qk", "pe_v")]
        pe_ctr, pe_cnt, pe_o, pe_log, pe_rank, pe_mxt = [sem(n) for n in ("pe_ctr", "pe_cnt", "pe_o", "pe_log", "pe_rank", "pe_mxt")]
        pe_s, pe_av, pe_m = sem("pe_s"), sem("pe_av"), sem("pe_m")
        a_exp_g, a_xn, a_xt, a_qkhi, a_v, a_exp, a_cx = [sem(n) for n in ("a_exp_g", "a_xn", "a_xt", "a_qkhi", "a_v", "a_exp", "a_cx")]
        a_ct, a_yn, a_x2, a_x2t, a_gex = [sem(n) for n in ("a_ct", "a_yn", "a_x2", "a_x2t", "a_gex")]
        v_gm, v_ga, v_h, v_st1, v_qklo, v_m, v_mxt = [sem(n) for n in ("v_gm", "v_ga", "v_h", "v_st1", "v_qklo", "v_m", "v_mxt")]
        v_cn, v_y, v_st2, v_st3, v_lg, v_gap, v_oh, v_slot, v_gate, v_rank = [sem(n) for n in (
            "v_cn", "v_y", "v_st2", "v_st3", "v_lg", "v_gap", "v_oh", "v_slot", "v_gate", "v_rank")]
        chain1, chain2, chain3, chain4, chain5 = [sem(f"chain{i}") for i in range(1, 6)]
        p_yg, p_kept, p_chain = sem("p_yg"), sem("p_kept"), sem("p_chain")
        plan_made, pads_sent = sem("plan_made"), sem("pads_sent")
        xs_in, w1_in, w2_in, bs_in, ye_out = sems("xs_in", 4), sems("w1_in"), sems("w2_in"), sems("bs_in", 4), sems("ye_out")
        b_xt, b_up, b_dn = sem("b_xt"), sem("b_up"), sem("b_dn")
        b_xhi, b_hhi, b_zn = sem("b_xhi"), sem("b_hhi"), sem("b_zn")
        b_xlo, b_hlo, b_z, b_st, b_dest = sem("b_xlo"), sem("b_hlo"), sem("b_z"), sem("b_st"), sem("b_dest")
        b_zg, b_ye = sem("b_zg"), sem("b_ye")
        p_st1, p_st2, p_st3, p_st4 = [sem(f"p_st{i}") for i in range(1, 5)]
        c_in, c_out, c_sum, c_chain = sems("c_in"), sems("c_out"), sem("c_sum"), sem("c_chain")

        block = ctx.enter_context(nc.Block())

        def settled(eng):
            eng.wait_ge(const_made, CONSTS)
        CONSTS = 11

        def phase_a(step):
            def run(loop, off):
                t = Pair(loop, off)
                pa, pb, pc = t, t.back(1), t.back(2)
                has = (lambda q: True) if loop is not None else (lambda q: 0 <= q.off < PAIRS)
                step(pa, pb, pc, has(pa), has(pb), has(pc))
            return run

        def run_phase_a(eng, step):
            run = phase_a(step)
            for t in range(4):
                run(None, t)
            with eng.Fori(0, (PAIRS - 4) // 2) as loop:
                run(loop, 4)
                run(loop, 5)
            for t in (PAIRS, PAIRS + 1):
                run(None, t)

        def run_phase_b(eng, step):
            def run(loop, off):
                t = Pair(loop, off, 4)
                has = (lambda q: True) if loop is not None else (lambda q: 0 <= q.off < GRID)
                step(t.back(-1), t, t.back(1), has(t.back(-1)), has(t), has(t.back(1)))
            for t in range(-1, 6):
                run(None, t)
            with eng.Fori(0, (GRID - 8) // 4) as loop:
                for u in range(4):
                    run(loop, 6 + u)
            for t in range(GRID - 2, GRID + 1):
                run(None, t)

        def run_phase_c(eng, step):
            for t in range(2):
                step(Pair(None, t))
            with eng.Fori(0, (PAIRS - 2) // 2) as loop:
                for u in range(2):
                    step(Pair(loop, 2 + u))

        @block.sync
        def _(sp):
            for dst, src in ((ncol[:, :], a["noise_cols"]), (nrow[:, :], a["noise_rows"]), (w12[:, :, :, :], a["w12"]),
                             (sw12[:, :, :, :], a["sw12"])):
                sp.dma_start(dst, src).then_inc(w_in, 16)
            for dst, src in ((w3[:, :], a["w3"]), (posb[:, :], a["pos"]), (b3r[:, :], a["b3"].to_broadcast([P, D])),
                             (wqkv[:, :, :], a["wqkv"]), (wo[:, :], a["wo"]), (lng[:, :], a["ln_gamma"].to_broadcast([P, D])),
                             (lnb[:, :], a["ln_beta"].to_broadcast([P, D])), (rw[:, :], a["router"])):
                sp.dma_start(dst, src).then_inc(wa_in, 16)

            def step(pa, pb, pc, has_a, has_b, has_c):
                if has_a:
                    if pa.exists:
                        wait(sp, p_kept, 1, pa.back(2), 1)
                        for i in range(2):
                            sp.dma_start(h[pa.par][:, 1 + i, :], a["txt"][bass.ds(pa.number * 2 + i, 1), :, :]
                                         .rearrange("a t d -> (a t) d")).then_inc(txt_in[pa.par], 16)
                    wait(sp, pe_tok, 1, pa.back(2), 1)
                    sp.dma_start(xin[pa.par][:, :, :], a["xp"][bass.ds(pa.number, 1), :, :, :]
                                 .rearrange("a p c t -> (a p) c t")).then_inc(xin_in[pa.par], 16)
                if has_c:
                    wait(sp, p_kept, 1, pc, 1)
                    wait(sp, v_gate, 1, pc, 1)
                    sp.dma_start(kept_d[bass.ds(pc.number, 1), :, :].rearrange("a p c -> (a p) c"),
                                 kept[pc.par][:, :, :].rearrange("p t c -> p (t c)")).then_inc(kept_out[pc.par], 16)
                if has_a:
                    wait(sp, v_qklo, 1, pa, 1)
                    wait(sp, a_qkhi, 1, pa, 1)
                    sp.dma_start(stack_d[pa.par].rearrange("s r t -> r s t"), kq[:, :, :]).then_inc(kq_out[pa.par], 16)
                    wait_dma(sp, kq_out, 1, pa)
                    wait(sp, pe_s, UNITS, pa.back(2), UNITS)
                    for dst, slots in ((kst[pa.par], (0, 1, 0)), (qst[pa.par], (2, 2, 3))):
                        for half in range(2):
                            for c in range(3):
                                src = stack_d[pa.par, slots[c]].rearrange("(j h r) t -> h r j t", j=4, h=2)[half]
                                at = 64 * half + 16 * c
                                sp.dma_start(dst[at:at + 16, :, :], src).then_inc(st_in[pa.par], 16)
                    wait(sp, v_mxt, 1, pa, 1)
                    for half in range(2):
                        at = 64 * half + 48
                        for j in range(4):
                            sp.dma_start(qst[pa.par][at:at + 1, j, :], mxT[4 * half + j:4 * half + j + 1, :]
                                         ).then_inc(max_in[pa.par], 16)

            run_phase_a(sp, step)

            sp.wait_ge(plan_made, 1)
            for i in range(2):
                sp.wait_ge(sent[i], 16 * 6 * (PAIRS // 2))
                sp.wait_ge(split_out[i], 16 * 2 * (NE // 2))
            sp.wait_ge(bsplit_out, 16 * 2)
            sp.wait_ge(pads_sent, 16 * (2 + 2 * NE))

            def load(g):
                row = sp.value_load(plan[0:1, 0, bass.ds(g.number, 1)], min_val=0, max_val=NE * CAP)
                wait(sp, b_z, 1, g.back(4), 1)
                wait(sp, b_dest, 1, g.back(4), 1)
                sp.dma_start(xs[g.slot][:, :, :], sorted_d[bass.ds(row, G), :].rearrange("(c p) d -> p c d", c=2)
                             ).then_inc(xs_in[g.slot], 16)

            def load_w(g):
                e = sp.value_load(plan[0:1, 1, bass.ds(g.number, 1)], min_val=0, max_val=NE - 1)
                wait(sp, b_up, 2, g.back(2), 2)
                sp.dma_start(w1s[g.par][:, :, :].rearrange("p s f -> p (s f)"),
                             w1_d[bass.ds(e, 1), :, :].rearrange("a p f -> (a p) f")).then_inc(w1_in[g.par], 16)
                wait(sp, b_dn, 1, g.back(4), 1)
                sp.dma_start(bs[g.slot][:, :], bias_d[bass.ds(e, 1), :, :].rearrange("a p f -> (a p) f")
                             ).then_inc(bs_in[g.slot], 16)
                wait(sp, b_dn, 1, g.back(2), 1)
                wait(sp, b_ye, 1, g.back(2), 1)
                wait(sp, b_dest, 1, g.back(2), 1)
                sp.dma_start(w2s[g.par][:, :].bitcast(I32), w2_d[bass.ds(e, 1), :, :].rearrange("a p f -> (a p) f")
                             ).then_inc(w2_in[g.par], 16)

            def step_b(nxt, cur, old, has_nxt, has_cur, has_old):
                if nxt.loop is None and nxt.off == 0:
                    load(nxt)
                    load_w(Pair(None, 0, 4))
                ahead = nxt.back(-1)
                if ahead.loop is not None or ahead.off < GRID:
                    load(ahead)
                if has_nxt and not (nxt.loop is None and nxt.off == 0):
                    load_w(nxt)

            run_phase_b(sp, step_b)

            for i in range(2):
                sp.wait_ge(ye_out[i], 16 * GRID)
                sp.wait_ge(kept_out[i], 16 * (PAIRS // 2))

            def load_c(q):
                wait(sp, c_sum, 1, q.back(2), 1)
                rows = expert_d.rearrange("(w g t p) d -> w g p t d", w=2, t=TILES, p=P)
                for w, dst in enumerate((y1, y2)):
                    sp.dma_start(dst[q.par][:, :, :], rows[w, bass.ds(q.number, 1), :, :, :]
                                 .rearrange("g p t d -> (g p) t d")).then_inc(c_in[q.par], 16)
                sp.dma_start(kc[q.par][:, :, :].rearrange("p t c -> p (t c)"),
                             kept_d[bass.ds(q.number, 1), :, :].rearrange("a p c -> (a p) c")).then_inc(c_in[q.par], 16)

            run_phase_c(sp, load_c)

        @block.scalar
        def _(act):
            act.wait_ge(w_in, 64)
            act.activation(nrow2[:, 0, :], nrow[:, :], ACT.Abs).then_inc(noise_root, 1)
            act.activation(ncol2[:, 4:6], ncol[:, 4:6], ACT.Abs).then_inc(noise_root, 1)
            act.wait_ge(noise_root, 2)
            act.activation(nrow2[:, 1, :], nrow2[:, 0, :], ACT.Sqrt).then_inc(noise_root, 1)
            act.activation(ncol2[:, 0:2], ncol2[:, 4:6], ACT.Sqrt).then_inc(noise_root, 1)

            def exps(pb, part):
                for n in range(3 * part, 3 * part + 3):
                    wait(act, pe_s, UNITS, pb, n + 1)
                    if n == 0:
                        wait(act, pe_av, 4, pb.back(1), 4)
                    act.activation(pex[n][:, :], bank[5 + n % 3][:, 0:COLS], ACT.Exp, scale=0.25).then_inc(a_exp, 1)

            def context(pb, g):
                wait(act, pe_av, 4, pb, 2 * g + 2)
                wait(act, pe_ctr, 2, pb.back(1), 2)
                act.activation(cx[g][:, 0:P].rearrange("p (b t) -> p b t", b=2), halves(bank[2][:, 0:COLS], PAT), ACT.Copy)
                act.activation(cx[g][:, P:COLS], bank[2][:, PAT:PAT + 2 * TXT], ACT.Copy).then_inc(a_cx, 1)

            def step(pa, pb, pc, has_a, has_b, has_c):
                if has_a:
                    wait(act, v_gm, 1, pa, 1)
                    act.activation(ge[:, :], gm[:, :], ACT.Exp).then_inc(a_exp_g, 1)
                if has_b:
                    exps(pb, 0)
                if has_c:
                    wait(act, p_st3, 2, pc, 2)
                    wait_dma(act, sent, 6, pc.back(2))
                    for k in range(TILES):
                        act.activation(pay[pc.par][:, k, 0:D], kept[pc.par][:, k, 0:D], ACT.Identity,
                                       bias=nm3[:, k:k + 1], scale=rs3[:, k:k + 1]).then_inc(a_x2, 1)
                    wait(act, pe_x2tr, 1, pc, 1)
                    wait(act, pe_log, 1, pc.back(1), 1)
                    act.activation(x2T[:, :], bank[0][:, 0:COLS], ACT.Copy).then_inc(a_x2t, 1)
                if has_b:
                    exps(pb, 1)
                if has_a:
                    wait(act, p_st1, 2, pa, 2)
                    wait(act, v_y, 1, pa.back(2), 1)
                    for k in range(TILES):
                        act.activation(xn[pa.par][:, k, :], h[pa.par][:, k, :], ACT.Identity,
                                       bias=nm1[:, k:k + 1], scale=rs1[:, k:k + 1]).then_inc(a_xn, 1)
                if has_b:
                    context(pb, 0)
                if has_a:
                    wait(act, pe_tr, 1, pa, 1)
                    wait(act, pe_v, 1, pa.back(1), 1)
                    act.activation(xT[:, :], bank[1][:, 0:COLS], ACT.Copy).then_inc(a_xt, 1)
                if has_b:
                    exps(pb, 2)
                if has_a:
                    wait_dma(act, kq_out, 1, pa.back(1))
                    for i in range(2):
                        wait(act, pe_qk, 2, pa, i + 1)
                        ins = act.activation(kq[:, 2 * (1 - i), :], bank[i][:, 0:COLS], ACT.Copy)
                        ins.then_inc(a_qkhi, 1)
                if has_c:
                    wait(act, v_gap, 1, pc, 1)
                    act.activation(gex[:, :], gap[:, :], ACT.Exp).then_inc(a_gex, 1)
                if has_a:
                    wait(act, pe_v, 1, pa, 1)
                    wait(act, pe_av, 4, pa.back(2), 4)
                    v = bank[1][:, 0:COLS].rearrange("p (t h r) -> p t h r", t=TILES, r=HD)
                    act.activation(vx[pa.par][:, 1:3, :, 0:HD], v[:, 1:3, :, :], ACT.Copy)
                    act.activation(vx[pa.par][0:PAT, 0, :, 0:HD], v[0:PAT, 0, :, :], ACT.Copy)
                    act.activation(vx[pa.par][PAT:P, 3, :, 0:HD], v[PAT:P, 0, :, :], ACT.Copy).then_inc(a_v, 1)
                if has_b:
                    exps(pb, 3)
                    context(pb, 1)
                    wait(act, pe_cnt, 1, pb, 1)
                    wait(act, pe_o, 1, pb.back(1), 1)
                    act.activation(cT[:, :], bank[1][:, 0:COLS], ACT.Copy).then_inc(a_ct, 1)
                    wait(act, p_st2, 2, pb, 2)
                    wait(act, p_yg, 1, pb.back(1), 1)
                    for k in range(TILES):
                        act.activation(yn[:, k, :], y[:, k, :], ACT.Identity,
                                       bias=nm2[:, k:k + 1], scale=rs2[:, k:k + 1]).then_inc(a_yn, 1)

            run_phase_a(act, step)

            def step_b(nxt, cur, old, has_nxt, has_cur, has_old):
                if has_nxt:
                    wait(act, b_xt, 1, nxt, 1)
                    wait(act, b_up, 2, nxt.back(2), 2)
                    act.activation(xsT[nxt.par][:, 0, :], bank[nxt.par][:, 0:G], ACT.Copy).then_inc(b_xhi, 1)
                if has_cur:
                    for i in range(2):
                        wait(act, b_up, 2, cur, i + 1)
                        wait(act, b_dn, 1, cur.back(2), 1)
                        act.activation(hid[cur.par][:, 0, 2 * i:2 * i + 2, :],
                                       bank[4 + 2 * cur.par + i][:, :].rearrange("p (c t) -> p c t", c=2),
                                       ACT.Relu).then_inc(b_hhi, 1)
                if has_old:
                    wait(act, p_st4, 2, old, 2)
                    wait(act, b_zg, 1, old.back(2), 1)
                    for k in range(2):
                        act.activation(zn[old.par][:, k, :], z[:, k, :], ACT.Identity,
                                       bias=nm4[old.par][:, k:k + 1], scale=rs4b[old.par][:, k:k + 1]).then_inc(b_zn, 1)

            run_phase_b(act, step_b)

            def store_c(q):
                wait(act, c_sum, 1, q, 1)
                for dst, src in ((out[bass.ds(q.number * 2, 1), 0:PAT, :], o2[q.par][0:PAT, 0, :]),
                                 (out[bass.ds(q.number * 2 + 1, 1), 0:PAT, :], o2[q.par][PAT:P, 0, :]),
                                 (out[bass.ds(q.number * 2, 1), PAT:SEQ, :], o2[q.par][:, 1, :]),
                                 (out[bass.ds(q.number * 2 + 1, 1), PAT:SEQ, :], o2[q.par][:, 2, :])):
                    act.dma_start(dst.rearrange("a t d -> (a t) d"), src).then_inc(c_out[q.par], 16)

            run_phase_c(act, store_c)
            for i in range(2):
                act.wait_ge(c_out[i], 16 * 4 * (PAIRS // 2))

        @block.tensor
        def _(pe):
            pe.wait_ge(const_made, CONSTS)
            pe.wait_ge(noise_row, 1)
            for w in range(2):
                for c in range(2):
                    last = pe.matmul(bank[0][:, (2 * c + w) * P:(2 * c + w + 1) * P],
                                     nrow2[:, 0, (2 * w + c) * P:(2 * w + c + 1) * P],
                                     nrow2[:, 0, 512 + w * P:512 + (w + 1) * P], start=True, stop=True)
            last.then_inc(noise_outer, 1)
            pe.wait_ge(noise_done, 1)
            pe.wait_ge(wa_in, 128)

            def scores(pb, part):
                k, q = kst[pb.par], qst[pb.par]
                for n in range(3 * part, 3 * part + 3):
                    half, js = unit(n)
                    rows = slice(64 * half, 64 * half + STACK)
                    free, last_read = (pb, n - 2) if n >= 3 else (pb.back(1), n + 10)
                    wait(pe, a_exp, UNITS, free, last_read, settled if len(js) == 2 else None)
                    s = bank[5 + n % 3]
                    for at, j in enumerate(js):
                        for b in range(2):
                            queries = q[rows, j, b * SEQ:(b + 1) * SEQ]
                            if len(js) == 1:
                                dst, keys = s[:, b * SEQ:(b + 1) * SEQ], k[rows, j, PAT + b * TXT:PAT + (b + 1) * TXT]
                            else:
                                dst = s[PAT * b:PAT * (b + 1), at * SEQ:(at + 1) * SEQ]
                                keys = k[rows, j, b * (COLS - PAT):b * (COLS - PAT) + PAT]
                            last = pe.matmul(dst, keys, queries, start=True, stop=True)
                    last.then_inc(pe_s, 1)

            def weigh(pb, j):
                first_unit = 6 * (j // 2)
                wait(pe, a_exp, UNITS, pb, first_unit + (6 if j % 2 else 4))
                if j % 2 == 0:
                    if j:
                        wait(pe, a_cx, 2, pb, 1)
                    else:
                        wait(pe, a_cx, 2, pb.back(1), 2)
                v = vx[pb.par]
                for b in range(2):
                    for part in range(2):
                        for half in range(2):
                            hd = 2 * j + half
                            q4 = 32 * (hd % 4)
                            dst = bank[2][q4:q4 + 32, b * SEQ:(b + 1) * SEQ]
                            if part == 0:
                                text = pex[first_unit + 4 * (j % 2) + half]
                                pe.matmul(dst, v[:, 1 + b, hd, :], text[:, b * SEQ:(b + 1) * SEQ], start=True, stop=False)
                            else:
                                patch = pex[first_unit + 2 + half]
                                last = pe.matmul(dst, v[:, 3 * b, hd, :], patch[:, (j % 2) * SEQ:(j % 2 + 1) * SEQ],
                                                 start=False, stop=True)
                last.then_inc(pe_av, 1)

            def maxima(pa, part):
                k, q = kst[pa.par], qst[pa.par]
                for n in range(3 * part, 3 * part + 3):
                    half, js = unit(n)
                    rows = slice(64 * half, 64 * half + STACK - 1)
                    free, last_read = (pa, n - 1) if n >= 2 else (pa.back(1), n + 11)
                    wait(pe, v_m, UNITS, free, last_read, settled if len(js) == 2 else None)
                    m = bank[3 + n % 2]
                    for at, j in enumerate(js):
                        for b in range(2):
                            keys = k[rows, j, b * SEQ:(b + 1) * SEQ]
                            if len(js) == 1:
                                dst, queries = m[:, b * SEQ:(b + 1) * SEQ], q[rows, j, PAT + b * TXT:PAT + (b + 1) * TXT]
                            else:
                                dst = m[PAT * b:PAT * (b + 1), at * SEQ:(at + 1) * SEQ]
                                queries = q[rows, j, b * (COLS - PAT):b * (COLS - PAT) + PAT]
                            last = pe.matmul(dst, queries, keys, start=True, stop=True)
                    last.then_inc(pe_m, 1)

            def step(pa, pb, pc, has_a, has_b, has_c):
                if has_a:
                    wait_dma(pe, xin_in, 1, pa)
                    wait(pe, v_y, 1, pa.back(2), 1)
                    for w in range(2):
                        for c in range(2):
                            last = pe.matmul(bank[0][:, w * P:(w + 1) * P], w12[:, c, w, :], xin[pa.par][:, c, :],
                                             start=(c == 0), stop=(c == 1))
                    last.then_inc(pe_tok, 1)
                if has_b:
                    wait_dma(pe, max_in, 8, pb)
                    wait(pe, a_v, 1, pb, 1)
                    scores(pb, 0)
                if has_a:
                    wait(pe, v_ga, 1, pa, 1)
                    wait(pe, v_mxt, 1, pa.back(1), 1)
                    pe.matmul(bank[1][:, 0:P], ga[:, :], w3[:, :], start=True, stop=True).then_inc(pe_w3, 1)
                if has_c:
                    wait(pe, a_x2, 3, pc, 3)
                    if has_a:
                        wait(pe, v_ga, 1, pa, 1)
                    if pc.loop is None and pc.off >= PAIRS - 2:
                        wait(pe, v_y, 1, pc, 1)
                        if has_b:
                            wait(pe, v_y, 1, pb.back(1), 1)
                    for k in range(TILES):
                        last = pe.transpose(bank[0][:, k * P:(k + 1) * P], pay[pc.par][:, k, 0:D], ident[:, :])
                    last.then_inc(pe_x2tr, 1)
                if has_b:
                    scores(pb, 1)
                if has_a:
                    wait(pe, a_xn, 3, pa, 3)
                    wait(pe, v_h, 1, pa, 1)
                    for k in range(TILES):
                        last = pe.transpose(bank[1][:, k * P:(k + 1) * P], xn[pa.par][:, k, :], ident[:, :])
                    last.then_inc(pe_tr, 1)
                if has_b:
                    weigh(pb, 0)
                    weigh(pb, 1)
                    scores(pb, 2)
                if has_a:
                    wait(pe, a_xt, 1, pa, 1)
                    if has_c:
                        wait(pe, a_x2t, 1, pc, 1)
                    else:
                        wait(pe, v_ga, 1, pa, 1)
                    for i in range(2):
                        pe.matmul(halves(bank[i][:, 0:COLS], PAT), wqkv[:, i, :], xT[:, 0:P], start=True, stop=True)
                        pe.matmul(bank[i][:, PAT:PAT + 2 * TXT], wqkv[:, i, :], xT[:, P:COLS], start=True,
                                  stop=True).then_inc(pe_qk, 1)
                if has_c:
                    wait(pe, a_x2t, 1, pc, 1)
                    if has_a:
                        wait(pe, v_qklo, 1, pa, 1)
                    for k in range(TILES):
                        last = pe.matmul(bank[0][:, k * NE:(k + 1) * NE], x2T[:, k * P:(k + 1) * P], rw[:, :],
                                         start=True, stop=True)
                    last.then_inc(pe_log, 1)
                if has_a:
                    wait(pe, v_qklo, 1, pa, 1)
                    for k in range(TILES):
                        last = pe.matmul(bank[1][:, k * P:(k + 1) * P], xT[:, k * P:(k + 1) * P], wqkv[:, 2, :],
                                         start=True, stop=True)
                    last.then_inc(pe_v, 1)
                if has_b:
                    scores(pb, 3)
                    weigh(pb, 2)
                if has_c:
                    wait(pe, v_oh, 1, pc, 1)
                    wait(pe, v_lg, 1, pc, 1)
                    for k in range(TILES):
                        for i in range(k + 1):
                            pe.matmul(bank[0][:, k * NE:(k + 1) * NE], before[:, :] if i == k else onesb[:, :],
                                      ohs[:, i, :], start=(i == 0), stop=(i == k))
                    for i in range(TILES):
                        last = pe.matmul(bank[0][:, TILES * NE:(TILES + 1) * NE], onesb[:, :], ohs[:, i, :],
                                         start=(i == 0), stop=(i == TILES - 1))
                    last.then_inc(pe_rank, 1)
                if has_b:
                    weigh(pb, 3)
                    if has_a:
                        wait(pe, a_v, 1, pa, 1)
                    wait(pe, a_cx, 2, pb, 2)
                    for k in (1, 2, 0):
                        if k == 0:
                            if has_c:
                                wait(pe, v_rank, 1, pc, 1)
                        for g in range(2):
                            dst = bank[1][:, (2 * (k - 1) + g) * P:(2 * (k - 1) + g + 1) * P] if k else \
                                bank[0][:, g * P:(g + 1) * P]
                            last = pe.transpose(dst, cx[g][:, k * P:(k + 1) * P], ident[:, :])
                        if k != 1:
                            last.then_inc(pe_ctr, 1)
                if has_a:
                    wait_dma(pe, st_in, 12, pa)
                    maxima(pa, 0)
                    maxima(pa, 1)
                if has_b:
                    wait(pe, v_cn, 1, pb, 1)
                    for k in range(TILES):
                        last = pe.transpose(bank[1][:, k * P:(k + 1) * P], cn[:, k, :], ident[:, :])
                    last.then_inc(pe_cnt, 1)
                if has_a:
                    maxima(pa, 2)
                if has_b:
                    wait(pe, a_ct, 1, pb, 1)
                    for k in range(TILES):
                        last = pe.matmul(bank[0][:, k * P:(k + 1) * P], cT[:, k * P:(k + 1) * P], wo[:, :],
                                         start=True, stop=True)
                    last.then_inc(pe_o, 1)
                if has_a:
                    maxima(pa, 3)
                    wait(pe, v_m, UNITS, pa, UNITS)
                    if has_b:
                        wait(pe, a_ct, 1, pb, 1)
                    else:
                        wait(pe, a_v, 1, pa, 1)
                    for k in range(TILES):
                        last = pe.transpose(tile_cols(bank[1][0:HEADS, 0:COLS], k),
                                            mx[:, k, :, :].rearrange("p a b -> p (a b)"), ident[:, :])
                    last.then_inc(pe_mxt, 1)

            run_phase_a(pe, step)

            ones2 = ones16x[0:2, :]

            def step_b(nxt, cur, old, has_nxt, has_cur, has_old):
                if has_nxt:
                    wait_dma(pe, xs_in, 1, nxt, 4)
                    wait(pe, b_xlo, 1, nxt.back(2), 1)
                    for k in range(2):
                        last = pe.transpose(bank[nxt.par][:, k * P:(k + 1) * P], xs[nxt.slot][:, k, 0:D], ident[:, :])
                    last.then_inc(b_xt, 1)
                if has_cur:
                    wait_dma(pe, w1_in, 1, cur)
                    wait_dma(pe, bs_in, 1, cur, 4)
                    wait(pe, b_xlo, 1, cur, 1)
                    wait(pe, b_xhi, 1, cur, 1)
                    w, x = w1s[cur.par], xsT[cur.par]
                    for i in range(2):
                        wait(pe, b_hlo, 2, cur.back(2), i + 1)
                        dst = bank[4 + 2 * cur.par + i]
                        for c in range(2):
                            f = (2 * i + c) * P
                            o = dst[:, c * G:(c + 1) * G]
                            pe.matmul(o, w[:, 0, f:f + P], x[:, 0, :], start=True, stop=False)
                            pe.matmul(o, w[:, 0, f:f + P], x[:, 1, :], start=False, stop=False)
                            pe.matmul(o, w[:, 1, f:f + P], x[:, 0, :], start=False, stop=False)
                            last = pe.matmul(o, bs[cur.slot][:, f:f + P], ones2[:, :], start=False, stop=True)
                        last.then_inc(b_up, 1)
                if has_old:
                    wait_dma(pe, w2_in, 1, old)
                    wait(pe, b_z, 1, old.back(2), 1)
                    wait(pe, b_hhi, 2, old, 2)
                    wait(pe, b_hlo, 2, old, 2)
                    w = w2s[old.par][:, 0:2 * F].rearrange("p (s c d) -> p s c d", s=2, c=FC)
                    hh = hid[old.par]
                    for k in range(2):
                        o = bank[2 + old.par][:, k * D:(k + 1) * D]
                        pe.matmul(o, ones2[:, 0:P], bs[old.slot][:, F:F + D], start=True, stop=False)
                        for c in range(FC):
                            pe.matmul(o, hh[:, 0, c, k * P:(k + 1) * P], w[:, 0, c, :], start=False, stop=False)
                            pe.matmul(o, hh[:, 0, c, k * P:(k + 1) * P], w[:, 1, c, :], start=False, stop=False)
                            last = pe.matmul(o, hh[:, 1, c, k * P:(k + 1) * P], w[:, 0, c, :], start=False,
                                             stop=(c == FC - 1))
                    last.then_inc(b_dn, 1)

            run_phase_b(pe, step_b)

        @block.vector
        def _(dve):
            for i in range(2):
                dve.memset(kst[i][32:64, :, :], MAXROW)
                dve.memset(kst[i][96:128, :, :], MAXROW)
                dve.memset(vx[i][PAT:P, 0, :, :], 0.0)
                dve.memset(vx[i][0:PAT, 3, :, :], 0.0)
                dve.memset(vx[i][0:PAT, 0, :, HD:2 * HD], 1.0)
                dve.memset(vx[i][:, 1:3, :, HD:2 * HD], 1.0)
                dve.memset(vx[i][PAT:P, 3, :, HD:2 * HD], 1.0).then_inc(const_made, 1)
            prep = Chain(dve, dve_prep, 6, Pair(None, 0))
            dve.wait_ge(w_in, 64)
            dve.wait_ge(noise_root, 4)
            dve.tensor_scalar(nrow2[:, 0, :], nrow[:, :], 0.0, None, ALU.is_lt)
            prep(dve.tensor_scalar(ncol2[:, 2:4], ncol[:, 4:6], 0.0, None, ALU.is_lt))
            dve.tensor_scalar(nrow2[:, 0, :], nrow2[:, 0, :], -2.0, 1.0, ALU.mult, ALU.add)
            prep(dve.tensor_scalar(ncol2[:, 2:4], ncol2[:, 2:4], -2.0, 1.0, ALU.mult, ALU.add))
            dve.tensor_tensor(nrow2[:, 0, :], nrow2[:, 0, :], nrow2[:, 1, :], ALU.mult).then_inc(noise_row, 1)
            prep(dve.tensor_tensor(ncol2[:, 0:2], ncol2[:, 0:2], ncol2[:, 2:4], ALU.mult))
            prep(dve.tensor_tensor(ncol2[:, 0:2], ncol2[:, 0:2], ncol[:, 2:4], ALU.mult))
            prep(dve.tensor_tensor(ncol2[:, 0:2], ncol2[:, 0:2], ncol[:, 0:2], ALU.add))
            dve.wait_ge(noise_outer, 1)
            prep(dve.tensor_tensor(sw12[:, :, :, :].rearrange("p a b c -> p (a b c)"),
                                   sw12[:, :, :, :].rearrange("p a b c -> p (a b c)"), bank[0][:, :], ALU.mult))
            prep.end()
            dve.wait_ge(wa_in, 128)
            dve.tensor_tensor(posb[:, :], posb[:, :], b3r[:, :], ALU.add)
            dve.tensor_tensor(w12[:, :, :, :].rearrange("p a b c -> p (a b c)"), w12[:, :, :, :]
                              .rearrange("p a b c -> p (a b c)"), sw12[:, :, :, :]
                              .rearrange("p a b c -> p (a b c)"), ALU.add).then_inc(noise_done, 1)
            dve.wait_ge(noise_done, 1)
            dve.wait_ge(const_made, CONSTS)

            def norm_stats(link, x, stat, mv, ve, eps, n, done, wait_free):
                for k in range(n):
                    ins = dve.bn_stats(stat[:, k, :], x(k))
                link(ins, settled)
                for k in range(n):
                    ins = dve.bn_aggr(mv[:, k, :], stat[:, k, :])
                link(ins)
                wait_free()
                dve.tensor_scalar(ve[:, 0, :], mv[:, :, 1], eps, None, ALU.add)
                dve.tensor_scalar(ve[:, 1, :], mv[:, :, 0], -1.0, None, ALU.mult).then_inc(done, 1)

            def reduce_max(pa, part):
                for n in range(3 * part, 3 * part + 3):
                    half, js = unit(n)
                    wait(dve, pe_m, UNITS, pa, n + 1)
                    if n == 0:
                        wait(dve, pe_mxt, 1, pa.back(1), 1)
                    dst = mx[:, 1:TILES, half, js[0]] if len(js) == 1 else mx[:, 0, half, js[0]:js[0] + 2]
                    dve.tensor_reduce(dst, bank[3 + n % 2][:, 0:COLS].rearrange("p (c s) -> p c s", c=2),
                                      AX.X, ALU.max).then_inc(v_m, 1)

            def step(pa, pb, pc, has_a, has_b, has_c):
                if has_a:
                    c1 = Chain(dve, chain1, 7, pa)
                    wait(dve, pe_tok, 1, pa, 1)
                    wait(dve, a_exp_g, 1, pa.back(1), 1)
                    dve.tensor_scalar(gm[:, :], bank[0][:, 0:P], ncol2[:, 0:1], 20.0, ALU.add, ALU.min).then_inc(v_gm, 1)
                if has_c:
                    c3 = Chain(dve, chain3, 11, pc)
                    wait(dve, p_kept, 1, pc, 1)
                    norm_stats(c3, lambda k: kept[pc.par][:, k, 0:D], stat3, mv3, ve3, EPS_LN, TILES,
                               v_st3, lambda: wait(dve, p_st3, 2, pc.back(1), 2))
                if has_a:
                    wait(dve, a_exp_g, 1, pa, 1)
                    c1(dve.scalar_tensor_tensor(out=gn[:, :], in0=ge[:, :], scalar=2.0, in1=ge[:, :], op0=ALU.add,
                                                op1=ALU.mult))
                    c1(dve.tensor_scalar(gg[:, :], gn[:, :], 2.0, None, ALU.add))
                    c1(dve.reciprocal(gr[:, :], gg[:, :]))
                    c1(dve.tensor_tensor(gt[:, :], gn[:, :], gr[:, :], ALU.mult))
                    c1(dve.scalar_tensor_tensor(out=gg[:, :], in0=bank[0][:, 0:P], scalar=ncol2[:, 0:1], in1=gt[:, :],
                                                op0=ALU.add, op1=ALU.mult))
                    wait(dve, pe_w3, 1, pa.back(1), 1)
                    dve.scalar_tensor_tensor(out=ga[:, :], in0=bank[0][:, P:2 * P], scalar=ncol2[:, 1:2], in1=gg[:, :],
                                             op0=ALU.add, op1=ALU.mult).then_inc(v_ga, 1)
                    wait(dve, pe_w3, 1, pa, 1)
                    wait(dve, p_kept, 1, pa.back(2), 1)
                    dve.tensor_tensor(h[pa.par][:, 0, :], bank[1][:, 0:P], posb[:, :], ALU.add).then_inc(v_h, 1)
                    wait(dve, v_h, 1, pa, 1)
                    wait_dma(dve, txt_in, 2, pa)
                    norm_stats(c1, lambda k: h[pa.par][:, k, :], stat1, mv1, ve1, EPS_LN, TILES, v_st1,
                               lambda: wait(dve, p_st1, 2, pa.back(1), 2))
                    wait(dve, a_qkhi, 2, pa, 1)
                    wait_dma(dve, kq_out, 1, pa.back(1))
                    dve.tensor_tensor(kq[:, 3, :], bank[0][:, 0:COLS], kq[:, 2, :], ALU.subtract)
                    wait(dve, a_qkhi, 2, pa, 2)
                    dve.tensor_tensor(kq[:, 1, :], bank[1][:, 0:COLS], kq[:, 0, :], ALU.subtract).then_inc(v_qklo, 1)
                    c1.end()
                if has_c:
                    wait(dve, pe_log, 1, pc, 1)
                    dve.tensor_copy(lg[:, :, :], bank[0][:, 0:TILES * NE].rearrange("p (t e) -> p t e", t=TILES)).then_inc(v_lg, 1)
                    wait(dve, v_lg, 1, pc, 1, settled)
                    for k in range(TILES):
                        ins = dve.max(top[:, k, :], lg[:, k, :])
                    c3(ins)
                    wait(dve, a_gex, 1, pc.back(1), 1)
                    dve.tensor_tensor(gap[:, :], top[:, :, 1], top[:, :, 0], ALU.subtract).then_inc(v_gap, 1)
                    for k in range(TILES):
                        ins = dve.max_index(topi[:, k, :], top[:, k, :], lg[:, k, :])
                    c3(ins)
                    c3(dve.tensor_copy(topf[:, :, :], topi[:, :, 0:2]))
                    i8 = iota8[:, :].unsqueeze(1).to_broadcast([P, TILES, NE])
                    dve.tensor_tensor(oh1[:, :, :], i8, topf[:, :, 0:1].to_broadcast([P, TILES, NE]), ALU.is_equal)
                    c3(dve.tensor_tensor(oh2[:, :, :], i8, topf[:, :, 1:2].to_broadcast([P, TILES, NE]), ALU.is_equal))
                    wait(dve, pe_rank, 1, pc.back(1), 1)
                    dve.tensor_tensor(ohs[:, :, :], oh1[:, :, :], oh2[:, :, :], ALU.add).then_inc(v_oh, 1)
                    wait_dma(dve, sent, 6, pc.back(2))
                    dve.tensor_copy(pay[pc.par][:, :, D], tok[:, :])
                    dve.tensor_copy(pay[pc.par][:, :, D + 1], topf[:, :, 0])
                    wait(dve, a_gex, 1, pc, 1)
                    wait_dma(dve, kept_out, 1, pc.back(2))
                    c3(dve.tensor_scalar(gsum[:, :], gex[:, :], 1.0, None, ALU.add))
                    c3(dve.reciprocal(kept[pc.par][:, :, D], gsum[:, :]))
                    dve.tensor_tensor(kept[pc.par][:, :, D + 1], gex[:, :], kept[pc.par][:, :, D], ALU.mult).then_inc(v_gate, 1)
                    dve.tensor_scalar(tok[:, :], tok[:, :], float(COLS), None, ALU.add)
                    wait(dve, pe_rank, 1, pc, 1)
                    c3(dve.tensor_tensor(rank[:, :, :], bank[0][:, 0:TILES * NE].rearrange("p (t e) -> p t e", t=TILES),
                                         base[:, :].unsqueeze(1).to_broadcast([P, TILES, NE]), ALU.add))
                    dve.tensor_tensor(base[:, :], base[:, :], bank[0][:, TILES * NE:(TILES + 1) * NE], ALU.add).then_inc(v_rank, 1)
                    dve.tensor_tensor(sl1[:, :, :], oh1[:, :, :], rank[:, :, :], ALU.mult)
                    c3(dve.tensor_tensor(sl2[:, :, :], oh2[:, :, :], rank[:, :, :], ALU.mult))
                    dve.tensor_reduce(slf[:, 0, :], sl1[:, :, :], AX.X, ALU.add)
                    c3(dve.tensor_reduce(slf[:, 1, :], sl2[:, :, :], AX.X, ALU.add))
                    dve.tensor_copy(slot[pc.par][:, :, :], slf[:, :, :]).then_inc(v_slot, 1)
                    c3.end()
                if has_b:
                    c2 = Chain(dve, chain2, 3, pb)
                    wait(dve, pe_ctr, 2, pb, 2)
                    views = []
                    for k in range(TILES):
                        t = bank[0][:, 0:2 * P] if k == 0 else bank[1][:, (k - 1) * 2 * P:k * 2 * P]
                        views.append(t.rearrange("p (h r) -> p h r", h=HEADS))
                    for k in range(TILES):
                        ins = dve.reciprocal(rden[:, k, :], views[k][:, :, HD])
                    c2(ins)
                    wait(dve, pe_cnt, 1, pb.back(1), 1)
                    for k in range(TILES):
                        ins = dve.tensor_tensor(cn[:, k, :].rearrange("p (h r) -> p h r", h=HEADS), views[k][:, :, 0:HD],
                                                rden[:, k, :].unsqueeze(2).to_broadcast([P, HEADS, HD]), ALU.mult)
                    ins.then_inc(v_cn, 1)
                if has_a:
                    reduce_max(pa, 0)
                    reduce_max(pa, 1)
                    reduce_max(pa, 2)
                if has_b:
                    wait(dve, pe_o, 1, pb, 1)
                    wait(dve, a_yn, 3, pb.back(1), 3)
                    ins = dve.tensor_tensor(y[:, :, :].rearrange("p t d -> p (t d)"), bank[0][:, 0:COLS],
                                            xn[pb.par][:, :, :].rearrange("p t d -> p (t d)"), ALU.add)
                    ins.then_inc(v_y, 1)
                    wait(dve, v_y, 1, pb, 1)
                    norm_stats(c2, lambda k: y[:, k, :], stat2, mv2, ve2, EPS_ATT, TILES, v_st2,
                               lambda: wait(dve, p_st2, 2, pb.back(1), 2))
                    c2.end()
                if has_a:
                    reduce_max(pa, 3)
                    wait(dve, pe_mxt, 1, pa, 1)
                    wait_dma(dve, max_in, 8, pa.back(1))
                    dve.tensor_scalar(mxT[:, :], bank[1][0:HEADS, 0:COLS], -1.0 / MAXROW, None, ALU.mult).then_inc(v_mxt, 1)

            run_phase_a(dve, step)

            link = Chain(dve, chain5, 12, Pair(None, 0))
            wait(dve, v_rank, 1, Pair(None, PAIRS - 1), 1)
            link(dve.tensor_tensor(cnt[:, :], base[:, :], ecap[:, :], ALU.subtract))
            link(dve.tensor_scalar(cnti[:, :], cnt[:, :], float(G - 1), None, ALU.add))
            link(dve.tensor_scalar(cntt[:, :], cnti[:, :], G.bit_length() - 1, None, ALU.arith_shift_right))
            link(dve.tensor_copy(ntl[:, :], cntt[:, :]))
            link(dve.tensor_tensor_scan(cum[:, :], one8[:, :], ntl[:, :], 0.0, ALU.mult, ALU.add))
            link(dve.tensor_tensor(past[:, :, :], iotag[:, :].unsqueeze(2).to_broadcast([P, GRID, NE]),
                                   cum[:, :].unsqueeze(1).to_broadcast([P, GRID, NE]), ALU.is_ge))
            dve.tensor_reduce(eg[:, :], past[:, :, :], AX.X, ALU.add)
            link(dve.tensor_tensor(pastn[:, :, :], past[:, :, :], ntl[:, :].unsqueeze(1).to_broadcast([P, GRID, NE]), ALU.mult))
            link(dve.tensor_reduce(cg[:, :], pastn[:, :, :], AX.X, ALU.add))
            link(dve.tensor_tensor(rg[:, :], iotag[:, :], cg[:, :], ALU.subtract))
            link(dve.tensor_scalar(rg2[:, :], rg[:, :], float(G), None, ALU.mult))
            link(dve.scalar_tensor_tensor(out=rg[:, :], in0=eg[:, :], scalar=float(CAP), in1=rg2[:, :], op0=ALU.mult, op1=ALU.add))
            dve.tensor_scalar(plan[:, 0, :], rg[:, :], float(NE * CAP), None, ALU.min)
            dve.tensor_scalar(plan[:, 1, :], eg[:, :], float(NE - 1), None, ALU.min)
            dve.tensor_scalar(padf[:, 0, :], base[:, :], lane[:, 0:1], None, ALU.add)
            link(dve.tensor_scalar(padf[:, 1, :], base[:, :], lane[:, 1:2], None, ALU.add))
            dve.tensor_copy(padi[:, :, :], padf[:, :, :]).then_inc(plan_made, 1)
            link.end()

            def step_b(nxt, cur, old, has_nxt, has_cur, has_old):
                if has_nxt:
                    wait(dve, b_xhi, 1, nxt, 1)
                    wait(dve, b_up, 2, nxt.back(2), 2)
                    dve.tensor_tensor(xsT[nxt.par][:, 1, :], bank[nxt.par][:, 0:G], xsT[nxt.par][:, 0, :],
                                      ALU.subtract).then_inc(b_xlo, 1)
                if has_old:
                    link = Chain(dve, chain4, 3, old)
                    wait(dve, b_dn, 1, old, 1)
                    wait(dve, b_zn, 2, old.back(1), 2)
                    dve.tensor_tensor(z[:, :, :], bank[2 + old.par][:, 0:2 * D].rearrange("p (c d) -> p c d", c=2),
                                      xs[old.slot][:, :, 0:D], ALU.add).then_inc(b_z, 1)
                    wait_dma(dve, w2_in, 1, old)
                    link(dve.tensor_scalar(first[:, :], xs[old.slot][:, :, D + 1],
                                           w2s[old.par][:, WROW2 - 2:WROW2].bitcast(F32), None, ALU.is_equal))
                    wait_dma(dve, ye_out, 2, old.back(2))
                    dve.scalar_tensor_tensor(out=dest[old.par][:, :], in0=first[:, :], scalar=-float(TOKENS),
                                             in1=xs[old.slot][:, :, D], op0=ALU.mult, op1=ALU.add).then_inc(b_dest, 1)
                if has_cur:
                    for i in range(2):
                        wait(dve, b_hhi, 2, cur, i + 1)
                        dve.scalar_tensor_tensor(out=hid[cur.par][:, 1, 2 * i:2 * i + 2, :].rearrange("p c t -> p (c t)"),
                                                 in0=bank[4 + 2 * cur.par + i][:, :], scalar=0.0,
                                                 in1=hid[cur.par][:, 0, 2 * i:2 * i + 2, :].rearrange("p c t -> p (c t)"),
                                                 op0=ALU.max, op1=ALU.subtract).then_inc(b_hlo, 1)
                        if has_old and i == 0:
                            for k in range(2):
                                ins = dve.bn_stats(stat4[:, k, :], z[:, k, :])
                            link(ins, settled)
                            for k in range(2):
                                ins = dve.bn_aggr(mv4[:, k, :], stat4[:, k, :])
                            link(ins)
                elif has_old:
                    for k in range(2):
                        ins = dve.bn_stats(stat4[:, k, :], z[:, k, :])
                    link(ins)
                    for k in range(2):
                        ins = dve.bn_aggr(mv4[:, k, :], stat4[:, k, :])
                    link(ins)
                if has_old:
                    wait(dve, p_st4, 2, old.back(1), 2)
                    dve.tensor_scalar(ve4[:, 0, :], mv4[:, :, 1], EPS_FFN, None, ALU.add)
                    dve.tensor_scalar(ve4[:, 1, :], mv4[:, :, 0], -1.0, None, ALU.mult).then_inc(b_st, 1)
                    link.end()

            run_phase_b(dve, step_b)

            def combine(q):
                wait(dve, c_sum, 1, q.back(2), 1)
                wait_dma(dve, c_in, 3, q)
                for k in range(TILES):
                    ins = dve.scalar_tensor_tensor(out=o1[q.par][:, k, :], in0=y1[q.par][:, k, :], scalar=kc[q.par][:, k, D:D + 1],
                                                   in1=kc[q.par][:, k, 0:D], op0=ALU.mult, op1=ALU.add)
                ins.then_inc(c_chain, 1)
                wait(dve, c_chain, 1, q, 1)
                wait_dma(dve, c_out, 4, q.back(2))
                for k in range(TILES):
                    ins = dve.scalar_tensor_tensor(out=o2[q.par][:, k, :], in0=y2[q.par][:, k, :],
                                                   scalar=kc[q.par][:, k, D + 1:D + 2], in1=o1[q.par][:, k, :],
                                                   op0=ALU.mult, op1=ALU.add)
                ins.then_inc(c_sum, 1)

            run_phase_c(dve, combine)

        @block.gpsimd
        def _(pool):
            pool.memset(ident[:, :], 0.0).then_inc(pool_prep, 1)
            pool.memset(before[:, :], 1.0).then_inc(pool_prep, 1)
            pool.wait_ge(pool_prep, 2)
            pool.affine_select(out=ident[:, :], in_=ident[:, :], compare_op=ALU.not_equal, fill=1.0, base=0,
                               pattern=[[-1, P]], channel_multiplier=1).then_inc(const_made, 1)
            pool.affine_select(out=before[:, :], in_=before[:, :], compare_op=ALU.is_gt, fill=0.0, base=0,
                               pattern=[[1, P]], channel_multiplier=-1).then_inc(const_made, 1)
            pool.memset(onesb[:, :], 1.0).then_inc(const_made, 1)
            pool.memset(ones16x[:, :], 1.0).then_inc(const_made, 1)
            pool.iota(iota8[:, :], [[1, NE]], base=0, channel_multiplier=0, allow_small_or_imprecise_dtypes=True).then_inc(const_made, 1)
            pool.iota(ecap[:, :], [[CAP, NE]], base=0, channel_multiplier=0, allow_small_or_imprecise_dtypes=True).then_inc(const_made, 1)
            pool.iota(base[:, :], [[CAP, NE]], base=0, channel_multiplier=0, allow_small_or_imprecise_dtypes=True).then_inc(const_made, 1)
            pool.iota(tok[:, :], [[P, TILES]], base=TOKENS, channel_multiplier=1, allow_small_or_imprecise_dtypes=True)
            pool.iota(iotag[:, :], [[1, GRID]], base=0, channel_multiplier=0, allow_small_or_imprecise_dtypes=True)
            pool.iota(lane[:, :], [[P, 2]], base=0, channel_multiplier=1, allow_small_or_imprecise_dtypes=True)
            pool.memset(one8[:, :], 1.0)
            pool.memset(neghalf[:, :], -0.5)
            for i in range(2):
                pool.memset(pay[i][:, :, D + 2:ROW], 0.0)
            pool.memset(padrow[:, 0:D], 0.0)
            pool.memset(padrow[:, D + 1:ROW], 0.0)
            pool.memset(padrow[:, D:D + 1], FAR).then_inc(const_made, 2)
            pool.wait_ge(const_made, CONSTS)
            for i in range(2):
                pool.dma_start(sorted_d[NE * CAP + i * P:NE * CAP + (i + 1) * P, :], padrow[:, :]).then_inc(pads_sent, 16)

            def fetch(e):
                i = e % 2
                if e >= 2:
                    pool.wait_ge(stage_used, e - 1)
                    pool.wait_ge(split_out[i], 16 * 2 * (e // 2))
                pool.dma_start(stage[i][:, 0, :], a["w1"][e]).then_inc(stage_in[i], 16)
                pool.dma_start(stage[i][:, 1, :].rearrange("p (c d) -> p c d", c=FC), a["w2"][e].rearrange("(c p) d -> p c d", p=P)
                               ).then_inc(stage_in[i], 16)
                gb = split2[i][:, 2 * F:2 * F + 4 * D].bitcast(F32)
                pool.dma_start(gb[:, 0:D], a["gamma"][e:e + 1, :].to_broadcast([P, D])).then_inc(stage_in[i], 16)
                pool.dma_start(gb[:, D:2 * D], a["beta"][e:e + 1, :].to_broadcast([P, D])).then_inc(stage_in[i], 16)

            for r in range(2):
                view = bstage[32 * r:32 * r + 1, :].rearrange("p (e c) -> p e c", e=NE)
                pool.dma_start(view[:, :, 0:F], a["b1"].unsqueeze(0)).then_inc(bstage_in, 16)
                pool.dma_start(view[:, :, F:F + D], a["b2"].unsqueeze(0)).then_inc(bstage_in, 16)
            fetch(0)
            fetch(1)
            pool.wait_ge(bstage_in, 64)
            for r in range(2):
                pool.tensor_copy(bsplit[32 * r:32 * r + 1, :], bstage[32 * r:32 * r + 1, :]).then_inc(bhi_made, 1)
            pool.wait_ge(bhi_made, 2)
            pool.tensor_tensor(bsplit[32:33, :], bstage[32:33, :], bsplit[32:33, :], ALU.subtract).then_inc(bsplit_made, 1)
            pool.wait_ge(bsplit_made, 1)
            for r in range(2):
                pool.dma_start(bias_d[:, r, :].unsqueeze(0), bsplit[32 * r:32 * r + 1, :].rearrange("p (e c) -> p e c", e=NE)
                               ).then_inc(bsplit_out, 16)
            for e in range(NE):
                i = e % 2
                pool.wait_ge(stage_in[i], 16 * 4 * (e // 2 + 1))
                pool.memset(split2[i][:, WROW2 - 2:WROW2].bitcast(F32), float(e))
                pool.tensor_copy(split1[i][:, 0:F], stage[i][:, 0, :])
                pool.tensor_copy(split2[i][:, 0:F], stage[i][:, 1, :]).then_inc(split_made, 1)
                pool.wait_ge(split_made, 2 * e + 1)
                pool.tensor_tensor(split1[i][:, F:2 * F], stage[i][:, 0, :], split1[i][:, 0:F], ALU.subtract)
                pool.tensor_tensor(split2[i][:, F:2 * F], stage[i][:, 1, :], split2[i][:, 0:F], ALU.subtract).then_inc(split_made, 1)
                pool.wait_ge(split_made, 2 * e + 2)
                pool.dma_start(w1_d[e], split1[i][:, :]).then_inc(split_out[i], 16)
                pool.dma_start(w2_d[e], split2[i][:, :].bitcast(I32)).then_inc(split_out[i], 16)
                if e + 2 < NE:
                    pool.wait_ge(split_out[i], 16 * 2 * (e // 2 + 1))
                    fetch2 = e + 2
                    pool.dma_start(stage[i][:, 0, :], a["w1"][fetch2]).then_inc(stage_in[i], 16)
                    pool.dma_start(stage[i][:, 1, :].rearrange("p (c d) -> p c d", c=FC),
                                   a["w2"][fetch2].rearrange("(c p) d -> p c d", p=P)).then_inc(stage_in[i], 16)
                    gb = split2[i][:, 2 * F:2 * F + 4 * D].bitcast(F32)
                    pool.dma_start(gb[:, 0:D], a["gamma"][fetch2:fetch2 + 1, :].to_broadcast([P, D])).then_inc(stage_in[i], 16)
                    pool.dma_start(gb[:, D:2 * D], a["beta"][fetch2:fetch2 + 1, :].to_broadcast([P, D])).then_inc(stage_in[i], 16)

            def scale_shift(made, per, item, ve, rs, nm, n, done, used):
                wait(pool, made, per, item, per)
                used()
                pool.tensor_tensor(rs, ve[:, 0, :], neghalf[:, 0:n], ALU.pow).then_inc(done, 1)
                wait(pool, done, 2, item, 1)
                pool.tensor_tensor(nm, ve[:, 1, :], rs, ALU.mult).then_inc(done, 1)

            def step(pa, pb, pc, has_a, has_b, has_c):
                if has_c:
                    scale_shift(v_st3, 1, pc, ve3, rs3[:, :], nm3[:, :], TILES, p_st3,
                                lambda: wait(pool, a_x2, 3, pc.back(1), 3))
                if has_a:
                    scale_shift(v_st1, 1, pa, ve1, rs1[:, :], nm1[:, :], TILES, p_st1,
                                lambda: wait(pool, a_xn, 3, pa.back(1), 3))
                if has_c:
                    wait(pool, v_slot, 1, pc, 1, settled)
                    for k in range(TILES):
                        for w in range(2):
                            pool.indirect_dma_start(
                                sorted_d[:, :], bass.IndirectOffsetOnAxis(ap=slot[pc.par][:, w, k:k + 1], axis=0),
                                pay[pc.par][:, k, :], None).then_inc(sent[pc.par], 16)
                if has_b:
                    scale_shift(v_st2, 1, pb, ve2, rs2[:, :], nm2[:, :], TILES, p_st2,
                                lambda: wait(pool, a_yn, 3, pb.back(1), 3))
                    wait(pool, a_yn, 3, pb, 3)
                    g3 = lng[:, :].unsqueeze(1).to_broadcast([P, TILES, D])
                    b3 = lnb[:, :].unsqueeze(1).to_broadcast([P, TILES, D])
                    pool.tensor_tensor(yg[:, :, :], yn[:, :, :], g3, ALU.mult).then_inc(p_yg, 1)
                    wait(pool, p_yg, 1, pb, 1)
                    pool.tensor_tensor(yg[:, :, :], yg[:, :, :], b3, ALU.add).then_inc(p_chain, 1)
                    wait(pool, p_chain, 1, pb, 1)
                    wait_dma(pool, kept_out, 1, pb.back(2))
                    pool.tensor_tensor(kept[pb.par][:, :, 0:D], yg[:, :, :], h[pb.par][:, :, :], ALU.add).then_inc(p_kept, 1)

            run_phase_a(pool, step)

            pool.wait_ge(plan_made, 1)
            for e in range(NE):
                for i in range(2):
                    pool.indirect_dma_start(sorted_d[:, :], bass.IndirectOffsetOnAxis(ap=padi[:, i, e:e + 1], axis=0),
                                            padrow[:, :], None).then_inc(pads_sent, 16)

            def step_b(nxt, cur, old, has_nxt, has_cur, has_old):
                if has_old:
                    scale_shift(b_st, 1, old, ve4, rs4b[old.par][:, :], nm4[old.par][:, :], 2, p_st4,
                                lambda: wait(pool, b_zn, 2, old.back(2), 2))
                    gb = w2s[old.par][:, 2 * F:2 * F + 4 * D].bitcast(F32)
                    wait(pool, b_zn, 2, old, 2)
                    pool.tensor_tensor(zg[:, :, :], zn[old.par][:, :, :], gb[:, 0:D].unsqueeze(1).to_broadcast([P, 2, D]),
                                       ALU.mult).then_inc(b_zg, 1)
                    wait(pool, b_zg, 1, old, 1)
                    wait_dma(pool, ye_out, 2, old.back(2))
                    pool.tensor_tensor(ye[old.par][:, :, :], zg[:, :, :], gb[:, D:2 * D].unsqueeze(1).to_broadcast([P, 2, D]),
                                       ALU.add).then_inc(b_ye, 1)
                    wait(pool, b_ye, 1, old, 1, settled)
                    wait(pool, b_dest, 1, old, 1)
                    for k in range(2):
                        pool.indirect_dma_start(expert_d[:, :], bass.IndirectOffsetOnAxis(ap=dest[old.par][:, k:k + 1], axis=0),
                                                ye[old.par][:, k, :], None, bounds_check=2 * TOKENS - 1, oob_is_err=False
                                                ).then_inc(ye_out[old.par], 16)

            run_phase_b(pool, step_b)


def kernel(**inputs):
    import numpy as _np
    import concourse.bacc as _bacc
    from concourse import mybir as _mybir
    from concourse.bass_utils import run_bass_kernel_spmd as _run

    i = {k.replace("L0_", ""): _np.asarray(v) for k, v in inputs.items()}
    xp = i["x"].reshape(PAIRS, 2, 8, 2, 8, 8, 16).transpose(0, 4, 6, 3, 1, 2, 5).reshape(PAIRS, P, 2, P)

    def both(u, v):
        return _np.stack([u.T.reshape(2, P, P), v.T.reshape(2, P, P)], axis=2).transpose(1, 0, 2, 3)

    at = _np.arange(PAT, dtype=_np.float32)[:, None] * _np.exp(
        _np.arange(0, D, 2, dtype=_np.float32) * _np.float32(-_np.log(10000.0) / D))
    table = _np.stack([_np.sin(at), _np.cos(at)], axis=-1).reshape(PAT, D)
    arrays = {
        "xp": xp, "txt": i["txt"],
        "w12": both(i["tok_W1_w"], i["tok_W2_w"]), "sw12": both(i["tok_W1_sw"], i["tok_W2_sw"]),
        "noise_rows": _np.concatenate([i["tok_eps_in1"], i["tok_eps_in2"], i["tok_eps_out1"], i["tok_eps_out2"]])[None, :],
        "noise_cols": _np.stack([i["tok_W1_b"], i["tok_W2_b"], i["tok_W1_sb"], i["tok_W2_sb"], i["tok_eps_out1"],
                                 i["tok_eps_out2"]], axis=1),
        "w3": i["tok_W3_w"].T, "b3": i["tok_W3_b"][None, :], "pos": _np.concatenate([table, table]),
        "wqkv": _np.stack([i["attn_W_q"].T, i["attn_W_k"].T, i["attn_W_v"].T], axis=1), "wo": i["attn_W_o"].T,
        "ln_gamma": i["attn_ln_gamma"][None, :], "ln_beta": i["attn_ln_beta"][None, :],
        "router": i["ffn_router_w"], "w1": i["ffn_w1"], "w2": i["ffn_w2"], "b1": i["ffn_b1"], "b2": i["ffn_b2"],
        "gamma": i["ffn_gamma"], "beta": i["ffn_beta"],
    }
    nc = _bacc.Bacc("TRN2", target_bir_lowering=False, num_devices=1)
    arrays = {f"in_{k}": _np.ascontiguousarray(v) for k, v in arrays.items()}
    args = {k[3:]: nc.dram_tensor(k, v.shape, _mybir.dt.from_np(v.dtype), kind="ExternalInput").ap()
            for k, v in arrays.items()}
    out = nc.dram_tensor("out_0", (IMAGES, SEQ, D), _mybir.dt.float32, kind="ExternalOutput").ap()
    early_fusion(nc, args, out)
    r = _run(nc, [arrays], core_ids=[0])
    return r.results[0]["out_0"]
```

```python
from contextlib import ExitStack

import numpy as np

import concourse.bass as bass
from concourse import mybir

ALU = mybir.AluOpType
ACT = mybir.ActivationFunctionType
AX = mybir.AxisListType
F32 = mybir.dt.float32
F16 = mybir.dt.float16
BF16 = mybir.dt.bfloat16
I32 = mybir.dt.int32
U32 = mybir.dt.uint32

P = 128
IMAGES, TXT, D = 32, 128, 128
PAT = 64
SEQ = PAT + TXT
COLS = 2 * SEQ
PAIRS = IMAGES // 2
TILES = COLS // P
TOKENS = IMAGES * SEQ
HEADS, HD = 8, 16
NE, F = 8, 512
FC = F // P
STACK = 49
MAXROW = 64.0
G = 256
GRID = 56
assert GRID >= 2 * TOKENS // G + NE - 1 and GRID % 4 == 0
CAP = TOKENS + G
ROW = 132
H2ROW = D + 2
WROW1, WROW2 = 2 * F, 2 * FC * D + 2 * 2 * D + 2
FAR = 1.0e6
EPS_ATT, EPS_FFN, EPS_LN = 1e-5, 1e-6, 1e-5


class Pair:

    def __init__(self, loop, off, unroll=2):
        self.loop, self.off, self.unroll = loop, off, unroll

    def back(self, n):
        return Pair(self.loop, self.off - n, self.unroll)

    @property
    def exists(self):
        return self.loop is not None or self.off >= 0

    @property
    def number(self):
        return self.off if self.loop is None else self.loop * self.unroll + self.off

    @property
    def par(self):
        return self.off % 2

    @property
    def slot(self):
        return self.off % 4

    def nth_of(self, ring):
        if self.loop is None:
            return self.off // ring
        return self.loop * (self.unroll // ring) + self.off // ring


def wait(eng, sem, per, pair, count, first_wait=None):
    if pair.exists:
        value = pair.number * per + count
        if first_wait and pair.loop is not None:
            eng.compute_val(value)
            first_wait(eng)
        eng.wait_ge(sem, value)


def wait_dma(eng, sems, per, pair, ring=2, first_wait=None):
    if pair.exists:
        value = pair.nth_of(ring) * (16 * per) + 16 * per
        if first_wait and pair.loop is not None:
            eng.compute_val(value)
            first_wait(eng)
        eng.wait_ge(sems[pair.off % ring], value)


class Chain:

    def __init__(self, eng, sem, per, pair):
        self.eng, self.sem, self.per, self.pair, self.n = eng, sem, per, pair, 0

    def __call__(self, ins, first_wait=None):
        self.n += 1
        ins.then_inc(self.sem, 1)
        value = self.pair.number * self.per + self.n
        if first_wait and self.pair.loop is not None:
            self.eng.compute_val(value)
            first_wait(self.eng)
        self.eng.wait_ge(self.sem, value)

    def end(self):
        assert self.n == self.per, (self.n, self.per)


UNITS = 12


def unit(n):
    group, i = divmod(n, 6)
    js = (2 * group, 2 * group + 1) if i in (2, 3) else (2 * group + i // 4,)
    return n % 2, js


def halves(ap2d, width):
    return bass.AP(ap2d.tensor, ap2d.offset, [list(ap2d.ap[0]), [COLS - PAT, 2], [1, width]])


def tile_cols(ap2d, k):
    if k == 0:
        return halves(ap2d, PAT)
    return ap2d[:, PAT + (k - 1) * TXT:PAT + k * TXT]


def early_fusion(nc, a, out):
    ctx = ExitStack()
    with ctx:
        def sb(name, shape, dt=F32):
            return ctx.enter_context(nc.sbuf_tensor(name, shape, dt))

        def sem(name):
            return ctx.enter_context(nc.semaphore(name))

        def sems(name, n=2):
            return [sem(f"{name}{i}") for i in range(n)]

        def dram(name, shape, dt=F32):
            return nc.dram_tensor(name, shape, dt).ap()

        bank = [ctx.enter_context(nc.psum_tensor(f"bank{i}", [P, 512], F32)) for i in range(8)]

        stack_d = dram("stack_d", [2, 6, P, COLS], F16)
        sorted_d = dram("sorted_d", [(NE + 1) * CAP, ROW])
        expert_d = dram("expert_d", [2 * TOKENS, D])
        kept_d = dram("kept_d", [PAIRS, P, TILES * H2ROW])
        w1_d = dram("w1_d", [NE, P, WROW1], F16)
        w2_d = dram("w2_d", [NE, P, WROW2 // 2], I32)
        bias_d = dram("bias_d", [NE, 2, F + D], F16)

        ident = sb("ident", [P, P])
        onesb = sb("onesb", [P, P], BF16)
        before = sb("before", [P, P], BF16)
        iota8 = sb("iota8", [P, NE])
        ecap = sb("ecap", [P, NE])
        iotag = sb("iotag", [P, GRID])
        w12 = sb("w12", [P, 2, 2, P])
        sw12 = sb("sw12", [P, 2, 2, P])
        nrow = sb("nrow", [1, 768])
        nrow2 = sb("nrow2", [1, 2, 768])
        ncol = sb("ncol", [P, 6])
        ncol2 = sb("ncol2", [P, 6])
        w3 = sb("w3", [P, P])
        posb = sb("posb", [P, D])
        b3r = sb("b3r", [P, D])
        wqkv = sb("wqkv", [P, 3, P])
        wo = sb("wo", [P, P])
        lng = sb("lng", [P, D])
        lnb = sb("lnb", [P, D])
        rw = sb("rw", [P, NE])
        stage = [sb(f"stage{i}", [P, F]) for i in range(2)]
        split1 = sb("split1", [P, WROW1], F16)
        split2 = sb("split2", [P, WROW2], F16)
        expert = sb("expert", [P, 1])
        bstage = sb("bstage", [64, NE * (F + D)])
        bsplit = sb("bsplit", [64, NE * (F + D)], F16)
        padrow = sb("padrow", [P, ROW])
        ones16x = sb("ones16x", [P, G], F16)
        lane = sb("lane", [P, 2])

        xin = [sb(f"xin{i}", [P, 2, P]) for i in range(2)]
        h = [sb(f"h{i}", [P, TILES, D]) for i in range(4)]
        gm = sb("gm", [P, P])
        ge = sb("ge", [P, P])
        gn = sb("gn", [P, P])
        gr = sb("gr", [P, P])
        gt = sb("gt", [P, P])
        gg = sb("gg", [P, P])
        ga = sb("ga", [P, P])
        stat1 = sb("stat1", [P, TILES, 6])
        mv1 = sb("mv1", [P, TILES, 2])
        ve1 = sb("ve1", [P, 2, TILES])
        rs1 = sb("rs1", [P, TILES])
        nm1 = sb("nm1", [P, TILES])
        xn = [sb(f"xn{i}", [P, TILES, D]) for i in range(2)]
        xT = sb("xT", [P, COLS])
        kq = sb("kq", [P, 4, COLS], F16)
        kst = [sb(f"kst{i}", [P, 4, COLS], F16) for i in range(2)]
        qst = [sb(f"qst{i}", [P, 4, COLS], F16) for i in range(2)]
        vx = [sb(f"vx{i}", [P, 4, HEADS, 2 * HD]) for i in range(2)]
        mx = sb("mx", [P, TILES, 2, 4])
        mxT = sb("mxT", [HEADS, COLS], F16)
        pex = [sb(f"pex{i}", [P, COLS]) for i in range(UNITS)]
        cx = [sb(f"cx{i}", [P, COLS]) for i in range(2)]
        rden = sb("rden", [P, TILES, HEADS])
        cn = sb("cn", [P, TILES, D])
        cT = sb("cT", [P, COLS])
        y = sb("y", [P, TILES, D])
        stat2 = sb("stat2", [P, TILES, 6])
        mv2 = sb("mv2", [P, TILES, 2])
        ve2 = sb("ve2", [P, 2, TILES])
        rs2 = sb("rs2", [P, TILES])
        nm2 = sb("nm2", [P, TILES])
        yn = sb("yn", [P, TILES, D])
        yg = sb("yg", [P, TILES, D])
        kept = [sb(f"kept{i}", [P, TILES, H2ROW]) for i in range(2)]
        stat3 = sb("stat3", [P, TILES, 6])
        mv3 = sb("mv3", [P, TILES, 2])
        ve3 = sb("ve3", [P, 2, TILES])
        rs3 = sb("rs3", [P, TILES])
        nm3 = sb("nm3", [P, TILES])
        pay = [sb(f"pay{i}", [P, TILES, ROW]) for i in range(2)]
        x2T = sb("x2T", [P, COLS])
        lg = sb("lg", [P, TILES, NE])
        top = sb("top", [P, TILES, 8])
        topi = sb("topi", [P, TILES, 8], U32)
        topf = sb("topf", [P, TILES, 2])
        gap = sb("gap", [P, TILES])
        gex = sb("gex", [P, TILES])
        gsum = sb("gsum", [P, TILES])
        oh1 = sb("oh1", [P, TILES, NE])
        oh2 = sb("oh2", [P, TILES, NE])
        ohs = sb("ohs", [P, TILES, NE], BF16)
        base = sb("base", [P, NE])
        rank = sb("rank", [P, TILES, NE])
        sl1 = sb("sl1", [P, TILES, NE])
        sl2 = sb("sl2", [P, TILES, NE])
        slf = sb("slf", [P, 2, TILES])
        slot = [sb(f"slot{i}", [P, 2, TILES], U32) for i in range(2)]
        tok = sb("tok", [P, TILES])

        cnt = sb("cnt", [P, NE])
        cnti = sb("cnti", [P, NE], I32)
        cntt = sb("cntt", [P, NE], I32)
        ntl = sb("ntl", [P, NE])
        one8 = sb("one8", [P, NE])
        cum = sb("cum", [P, NE])
        past = sb("past", [P, GRID, NE])
        pastn = sb("pastn", [P, GRID, NE])
        eg = sb("eg", [P, GRID])
        cg = sb("cg", [P, GRID])
        rg = sb("rg", [P, GRID])
        rg2 = sb("rg2", [P, GRID])
        plan = sb("plan", [P, 2, GRID], I32)
        padf = sb("padf", [P, 2, NE])
        padi = sb("padi", [P, 2, NE], U32)

        xs = [sb(f"xs{i}", [P, 2, ROW]) for i in range(4)]
        w1s = [sb(f"w1s{i}", [P, 2, F], F16) for i in range(4)]
        w2s = [sb(f"w2s{i}", [P, WROW2], F16) for i in range(4)]
        bs = [sb(f"bs{i}", [2, F + D], F16) for i in range(4)]
        xsT = [sb(f"xsT{i}", [P, 2, G], F16) for i in range(2)]
        hid = [sb(f"hid{i}", [P, 2, FC, G], F16) for i in range(2)]
        z = [sb(f"z{i}", [P, 2, D]) for i in range(2)]
        stat4 = sb("stat4", [P, 2, 6])
        mv4 = sb("mv4", [P, 2, 2])
        ve4 = sb("ve4", [P, 2, 2])
        neghalf = sb("neghalf", [P, TILES])
        nm4 = [sb(f"nm4_{i}", [P, 2]) for i in range(2)]
        rs4b = [sb(f"rs4b_{i}", [P, 2]) for i in range(2)]
        zn = [sb(f"zn{i}", [P, 2, D]) for i in range(2)]
        zg = sb("zg", [P, 2, D])
        ye = [sb(f"ye{i}", [P, 2, D]) for i in range(2)]
        first = sb("first", [P, 2])
        dest = [sb(f"dest{i}", [P, 2], U32) for i in range(4)]

        y1 = [sb(f"y1_{i}", [P, TILES, D]) for i in range(2)]
        y2 = [sb(f"y2_{i}", [P, TILES, D]) for i in range(2)]
        kc = [sb(f"kc{i}", [P, TILES, H2ROW]) for i in range(2)]
        o1 = [sb(f"o1_{i}", [P, TILES, D]) for i in range(2)]
        o2 = [sb(f"o2_{i}", [P, TILES, D]) for i in range(2)]

        w_in, wa_in = sem("w_in"), sem("wa_in")
        stage_in, split_out = sems("stage_in"), sems("split_out")
        split_made = sem("split_made")
        bstage_in, bhi_made, bsplit_made, bsplit_out = sem("bstage_in"), sem("bhi_made"), sem("bsplit_made"), sem("bsplit_out")
        const_made, pool_prep, dve_prep = sem("const_made"), sem("pool_prep"), sem("dve_prep")
        noise_root, noise_row, noise_outer, noise_done = sem("noise_root"), sem("noise_row"), sem("noise_outer"), sem("noise_done")
        xin_in, txt_in = sems("xin_in"), sems("txt_in")
        kq_out, st_in, max_in, kept_out, sent = sems("kq_out"), sems("st_in"), sems("max_in"), sems("kept_out"), sems("sent")
        pe_tok, pe_w3, pe_tr, pe_x2tr, pe_qk, pe_v = [sem(n) for n in ("pe_tok", "pe_w3", "pe_tr", "pe_x2tr", "pe_qk", "pe_v")]
        pe_ctr, pe_cnt, pe_o, pe_log, pe_rank, pe_mxt = [sem(n) for n in ("pe_ctr", "pe_cnt", "pe_o", "pe_log", "pe_rank", "pe_mxt")]
        pe_s, pe_av, pe_m = sem("pe_s"), sem("pe_av"), sem("pe_m")
        a_exp_g, a_xn, a_xt, a_qkhi, a_v, a_exp, a_cx = [sem(n) for n in ("a_exp_g", "a_xn", "a_xt", "a_qkhi", "a_v", "a_exp", "a_cx")]
        a_ct, a_yn, a_x2, a_x2t, a_gex = [sem(n) for n in ("a_ct", "a_yn", "a_x2", "a_x2t", "a_gex")]
        v_gm, v_ga, v_h, v_st1, v_qklo, v_m, v_mxt = [sem(n) for n in ("v_gm", "v_ga", "v_h", "v_st1", "v_qklo", "v_m", "v_mxt")]
        v_cn, v_y, v_st2, v_st3, v_lg, v_gap, v_oh, v_slot, v_gate, v_rank = [sem(n) for n in (
            "v_cn", "v_y", "v_st2", "v_st3", "v_lg", "v_gap", "v_oh", "v_slot", "v_gate", "v_rank")]
        chain1, chain2, chain3, chain4, chain5 = [sem(f"chain{i}") for i in range(1, 6)]
        p_yg, p_kept, p_chain = sem("p_yg"), sem("p_kept"), sem("p_chain")
        plan_made, pads_sent = sem("plan_made"), sem("pads_sent")
        xs_in, w1_in, w2_in, bs_in, ye_out = sems("xs_in", 4), sems("w1_in", 4), sems("w2_in", 4), sems("bs_in", 4), sems("ye_out")
        b_xt, b_up, b_dn = sem("b_xt"), sem("b_up"), sem("b_dn")
        b_xhi, b_hhi, b_zn = sem("b_xhi"), sem("b_hhi"), sem("b_zn")
        b_xlo, b_hlo, b_z, b_st, b_dest = sem("b_xlo"), sem("b_hlo"), sem("b_z"), sem("b_st"), sem("b_dest")
        b_zg, b_ye = sem("b_zg"), sem("b_ye")
        p_st1, p_st2, p_st3, p_st4 = [sem(f"p_st{i}") for i in range(1, 5)]
        c_in, c_out, c_sum, c_chain = sems("c_in"), sems("c_out"), sem("c_sum"), sem("c_chain")

        block = ctx.enter_context(nc.Block())

        def settled(eng):
            eng.wait_ge(const_made, CONSTS)
        CONSTS = 11

        def phase_a(step):
            def run(loop, off):
                t = Pair(loop, off, 4)
                pa, pb, pc = t, t.back(1), t.back(2)
                has = (lambda q: True) if loop is not None else (lambda q: 0 <= q.off < PAIRS)
                step(pa, pb, pc, has(pa), has(pb), has(pc))
            return run

        def run_phase_a(eng, step):
            run = phase_a(step)
            for t in range(4):
                run(None, t)
            with eng.Fori(0, (PAIRS - 8) // 4) as loop:
                for u in range(4):
                    run(loop, 4 + u)
            for t in range(PAIRS - 4, PAIRS + 2):
                run(None, t)

        def run_phase_b(eng, step):
            def run(loop, off):
                t = Pair(loop, off, 4)
                has = (lambda q: True) if loop is not None else (lambda q: 0 <= q.off < GRID)
                step(t.back(-1), t, t.back(1), has(t.back(-1)), has(t), has(t.back(1)))
            for t in range(-1, 6):
                run(None, t)
            with eng.Fori(0, (GRID - 8) // 4) as loop:
                for u in range(4):
                    run(loop, 6 + u)
            for t in range(GRID - 2, GRID + 1):
                run(None, t)

        def run_phase_c(eng, step):
            for t in range(2):
                step(Pair(None, t))
            with eng.Fori(0, (PAIRS - 2) // 2) as loop:
                for u in range(2):
                    step(Pair(loop, 2 + u))

        @block.sync
        def _(sp):
            for dst, src in ((ncol[:, :], a["noise_cols"]), (nrow[:, :], a["noise_rows"]), (w12[:, :, :, :], a["w12"]),
                             (sw12[:, :, :, :], a["sw12"])):
                sp.dma_start(dst, src).then_inc(w_in, 16)
            for dst, src in ((w3[:, :], a["w3"]), (posb[:, :], a["pos"]), (b3r[:, :], a["b3"].to_broadcast([P, D])),
                             (wqkv[:, :, :], a["wqkv"]), (wo[:, :], a["wo"]), (lng[:, :], a["ln_gamma"].to_broadcast([P, D])),
                             (lnb[:, :], a["ln_beta"].to_broadcast([P, D])), (rw[:, :], a["router"])):
                sp.dma_start(dst, src).then_inc(wa_in, 16)

            def load_patches(q):
                wait(sp, pe_tok, 1, q.back(2), 1)
                sp.dma_start(xin[q.par][:, :, :], a["xp"][bass.ds(q.number, 1), :, :, :]
                             .rearrange("a p c t -> (a p) c t")).then_inc(xin_in[q.par], 16)

            def load_texts(q):
                wait(sp, p_kept, 1, q.back(4), 1)
                for i in range(2):
                    sp.dma_start(h[q.slot][:, 1 + i, :], a["txt"][bass.ds(q.number * 2 + i, 1), :, :]
                                 .rearrange("a t d -> (a t) d")).then_inc(txt_in[q.par], 16)

            def load_weights(q):
                e = bass.ds(q.nth_of(2), 1)
                wait(sp, split_made, 2, q.back(2), 2, settled)
                if q.par == 0:
                    sp.dma_start(stage[0][:, :], a["w1"][e].rearrange("a p f -> (a p) f")).then_inc(stage_in[0], 16)
                else:
                    sp.dma_start(stage[1][:, :].rearrange("p (c d) -> p c d", c=FC),
                                 a["w2"][e].rearrange("a (c p) d -> (a p) c d", p=P)).then_inc(stage_in[1], 16)
                    wait_dma(sp, split_out, 1, q.back(2), 2, settled)
                    gb = split2[:, 2 * F:2 * F + 4 * D].bitcast(F32)
                    sp.dma_start(gb[:, 0:D], a["gamma"][e, :].to_broadcast([P, D])).then_inc(stage_in[1], 16)
                    sp.dma_start(gb[:, D:2 * D], a["beta"][e, :].to_broadcast([P, D])).then_inc(stage_in[1], 16)

            def store_weights(q):
                wait(sp, split_made, 2, q, 2, settled)
                src, dst = (split1[:, :], w1_d) if q.par == 0 else (split2[:, :].bitcast(I32), w2_d)
                sp.dma_start(dst[bass.ds(q.nth_of(2), 1), :, :].rearrange("a p f -> (a p) f"), src
                             ).then_inc(split_out[q.par], 16)

            def step(pa, pb, pc, has_a, has_b, has_c):
                ahead = pa.back(-1)
                if pa.loop is None and pa.off == 0:
                    load_texts(pa)
                    load_patches(pa)
                if has_a:
                    load_weights(pa)
                if ahead.loop is not None or ahead.off < PAIRS:
                    load_patches(ahead)
                    load_texts(ahead)
                if has_a:
                    wait(sp, v_qklo, 1, pa, 1, settled)
                    wait(sp, a_qkhi, 2, pa, 2)
                    planes = stack_d[pa.par]
                    sp.dma_start(planes[1:5].rearrange("c r t -> r c t"), kq[:, :, :]).then_inc(kq_out[pa.par], 16)
                    sp.dma_start(planes[0:6:5].rearrange("c r t -> r c t"), kq[:, 0:4:3, :]).then_inc(kq_out[pa.par], 16)
                    wait_dma(sp, kq_out, 2, pa)
                    wait(sp, pe_s, UNITS, pa.back(2), UNITS)
                    for side, dst in enumerate((kst[pa.par], qst[pa.par])):
                        for half in range(2):
                            src = planes[3 * side:3 * side + 3].rearrange("c (r h j) t -> h (c r) (j t)", h=2, j=4)[half]
                            sp.dma_start(dst[64 * half:64 * half + 48, :, :].rearrange("p j t -> p (j t)"), src
                                         ).then_inc(st_in[pa.par], 16)
                if has_c:
                    wait(sp, p_kept, 1, pc, 1)
                    wait(sp, v_gate, 1, pc, 1)
                    sp.dma_start(kept_d[bass.ds(pc.number, 1), :, :].rearrange("a p c -> (a p) c"),
                                 kept[pc.par][:, :, :].rearrange("p t c -> p (t c)")).then_inc(kept_out[pc.par], 16)
                if has_a:
                    store_weights(pa)
                    wait(sp, v_mxt, 1, pa, 1)
                    for half in range(2):
                        at = 64 * half + 48
                        for j in range(4):
                            sp.dma_start(qst[pa.par][at:at + 1, j, :], mxT[4 * half + j:4 * half + j + 1, :]
                                         ).then_inc(max_in[pa.par], 16)

            run_phase_a(sp, step)

            sp.wait_ge(plan_made, 1)
            for i in range(2):
                sp.wait_ge(sent[i], 16 * 6 * (PAIRS // 2))
                sp.wait_ge(split_out[i], 16 * NE)
            sp.wait_ge(bsplit_out, 16 * 2)
            sp.wait_ge(pads_sent, 16 * (2 + 2 * NE))

            def load(g):
                row = sp.value_load(plan[0:1, 0, bass.ds(g.number, 1)], min_val=0, max_val=NE * CAP)
                wait(sp, b_z, 1, g.back(4), 1)
                wait(sp, b_dest, 1, g.back(4), 1)
                sp.dma_start(xs[g.slot][:, :, :], sorted_d[bass.ds(row, G), :].rearrange("(c p) d -> p c d", c=2)
                             ).then_inc(xs_in[g.slot], 16)

            def load_w(g):
                e = sp.value_load(plan[0:1, 1, bass.ds(g.number, 1)], min_val=0, max_val=NE - 1)
                wait(sp, b_up, 2, g.back(4), 2)
                sp.dma_start(w1s[g.slot][:, :, :].rearrange("p s f -> p (s f)"),
                             w1_d[bass.ds(e, 1), :, :].rearrange("a p f -> (a p) f")).then_inc(w1_in[g.slot], 16)
                wait(sp, b_dn, 1, g.back(4), 1)
                sp.dma_start(bs[g.slot][:, :], bias_d[bass.ds(e, 1), :, :].rearrange("a p f -> (a p) f")
                             ).then_inc(bs_in[g.slot], 16)

            def load_w2(g):
                e = sp.value_load(plan[0:1, 1, bass.ds(g.number, 1)], min_val=0, max_val=NE - 1)
                wait(sp, b_ye, 1, g.back(4), 1)
                sp.dma_start(w2s[g.slot][:, :].bitcast(I32), w2_d[bass.ds(e, 1), :, :].rearrange("a p f -> (a p) f")
                             ).then_inc(w2_in[g.slot], 16)

            def step_b(nxt, cur, old, has_nxt, has_cur, has_old):
                if nxt.loop is None and nxt.off == 0:
                    load(nxt)
                    load_w(nxt)
                ahead = nxt.back(-1)
                if ahead.loop is not None or ahead.off < GRID:
                    load(ahead)
                    load_w(ahead)
                if has_nxt:
                    load_w2(nxt)

            run_phase_b(sp, step_b)

            for i in range(2):
                sp.wait_ge(ye_out[i], 16 * GRID)
                sp.wait_ge(kept_out[i], 16 * (PAIRS // 2))

            def load_c(q):
                wait(sp, c_sum, 1, q.back(2), 1)
                rows = expert_d.rearrange("(w g t p) d -> w g p t d", w=2, t=TILES, p=P)
                for w, dst in enumerate((y1, y2)):
                    sp.dma_start(dst[q.par][:, :, :], rows[w, bass.ds(q.number, 1), :, :, :]
                                 .rearrange("g p t d -> (g p) t d")).then_inc(c_in[q.par], 16)
                sp.dma_start(kc[q.par][:, :, :].rearrange("p t c -> p (t c)"),
                             kept_d[bass.ds(q.number, 1), :, :].rearrange("a p c -> (a p) c")).then_inc(c_in[q.par], 16)

            run_phase_c(sp, load_c)

        @block.scalar
        def _(act):
            act.wait_ge(w_in, 64)
            act.activation(nrow2[:, 0, :], nrow[:, :], ACT.Abs).then_inc(noise_root, 1)
            act.activation(ncol2[:, 4:6], ncol[:, 4:6], ACT.Abs).then_inc(noise_root, 1)
            act.wait_ge(noise_root, 2)
            act.activation(nrow2[:, 1, :], nrow2[:, 0, :], ACT.Sqrt).then_inc(noise_root, 1)
            act.activation(ncol2[:, 0:2], ncol2[:, 4:6], ACT.Sqrt).then_inc(noise_root, 1)

            def exps(pb, part):
                for n in range(3 * part, 3 * part + 3):
                    wait(act, pe_s, UNITS, pb, n + 1)
                    if n == 0:
                        wait(act, pe_av, 4, pb.back(1), 4)
                    act.activation(pex[n][:, :], bank[5 + n % 3][:, 0:COLS], ACT.Exp, scale=0.25).then_inc(a_exp, 1)

            def context(pb, g):
                wait(act, pe_av, 4, pb, 2 * g + 2)
                wait(act, pe_ctr, 2, pb.back(1), 2)
                act.activation(cx[g][:, 0:P].rearrange("p (b t) -> p b t", b=2), halves(bank[2][:, 0:COLS], PAT), ACT.Copy)
                act.activation(cx[g][:, P:COLS], bank[2][:, PAT:PAT + 2 * TXT], ACT.Copy).then_inc(a_cx, 1)

            def step(pa, pb, pc, has_a, has_b, has_c):
                if has_a:
                    wait(act, v_gm, 1, pa, 1)
                    act.activation(ge[:, :], gm[:, :], ACT.Exp).then_inc(a_exp_g, 1)
                if has_b:
                    exps(pb, 0)
                if has_a:
                    wait(act, p_st1, 2, pa, 2)
                    wait(act, v_y, 1, pa.back(2), 1)
                    for k in range(TILES):
                        act.activation(xn[pa.par][:, k, :], h[pa.slot][:, k, :], ACT.Identity,
                                       bias=nm1[:, k:k + 1], scale=rs1[:, k:k + 1]).then_inc(a_xn, 1)
                    wait(act, pe_tr, 1, pa, 1)
                    wait(act, pe_v, 1, pa.back(1), 1)
                    act.activation(xT[:, :], bank[1][:, 0:COLS], ACT.Copy).then_inc(a_xt, 1)
                    wait_dma(act, kq_out, 2, pa.back(1))
                    for i in range(2):
                        wait(act, pe_qk, 2, pa, i + 1)
                        ins = act.activation(kq[:, 3 * (1 - i), :], bank[i][:, 0:COLS], ACT.Copy)
                        ins.then_inc(a_qkhi, 1)
                if has_b:
                    exps(pb, 1)
                if has_a:
                    wait(act, pe_v, 1, pa, 1)
                    wait(act, pe_av, 4, pa.back(2), 4)
                    v = bank[1][:, 0:COLS].rearrange("p (t h r) -> p t h r", t=TILES, r=HD)
                    act.activation(vx[pa.par][:, 1:3, :, 0:HD], v[:, 1:3, :, :], ACT.Copy)
                    act.activation(vx[pa.par][0:PAT, 0, :, 0:HD], v[0:PAT, 0, :, :], ACT.Copy)
                    act.activation(vx[pa.par][PAT:P, 3, :, 0:HD], v[PAT:P, 0, :, :], ACT.Copy).then_inc(a_v, 1)
                if has_c:
                    wait(act, p_st3, 2, pc, 2)
                    wait_dma(act, sent, 6, pc.back(2))
                    for k in range(TILES):
                        act.activation(pay[pc.par][:, k, 0:D], kept[pc.par][:, k, 0:D], ACT.Identity,
                                       bias=nm3[:, k:k + 1], scale=rs3[:, k:k + 1]).then_inc(a_x2, 1)
                    wait(act, pe_x2tr, 1, pc, 1)
                    wait(act, pe_log, 1, pc.back(1), 1)
                    act.activation(x2T[:, :], bank[0][:, 0:COLS], ACT.Copy).then_inc(a_x2t, 1)
                if has_b:
                    exps(pb, 2)
                    context(pb, 0)
                if has_c:
                    wait(act, v_gap, 1, pc, 1)
                    act.activation(gex[:, :], gap[:, :], ACT.Exp).then_inc(a_gex, 1)
                if has_b:
                    exps(pb, 3)
                    context(pb, 1)
                    wait(act, pe_cnt, 1, pb, 1)
                    wait(act, pe_o, 1, pb.back(1), 1)
                    act.activation(cT[:, :], bank[1][:, 0:COLS], ACT.Copy).then_inc(a_ct, 1)
                    wait(act, p_st2, 2, pb, 2)
                    wait(act, p_yg, 1, pb.back(1), 1)
                    for k in range(TILES):
                        act.activation(yn[:, k, :], y[:, k, :], ACT.Identity,
                                       bias=nm2[:, k:k + 1], scale=rs2[:, k:k + 1]).then_inc(a_yn, 1)

            run_phase_a(act, step)

            def normalise(q):
                wait(act, p_st4, 2, q, 2)
                wait(act, b_zg, 1, q.back(2), 1)
                for k in range(2):
                    act.activation(zn[q.par][:, k, :], z[q.par][:, k, :], ACT.Identity,
                                   bias=nm4[q.par][:, k:k + 1], scale=rs4b[q.par][:, k:k + 1]).then_inc(b_zn, 1)

            def step_b(nxt, cur, old, has_nxt, has_cur, has_old):
                before = old.back(1)
                if has_nxt:
                    wait(act, b_xt, 1, nxt, 1)
                    wait(act, b_up, 2, nxt.back(2), 2)
                    act.activation(xsT[nxt.par][:, 0, :], bank[nxt.par][:, 0:G], ACT.Copy).then_inc(b_xhi, 1)
                if before.loop is not None or before.off >= 0:
                    normalise(before)
                if has_cur:
                    for i in range(2):
                        wait(act, b_up, 2, cur, i + 1)
                        wait(act, b_dn, 1, cur.back(2), 1)
                        act.activation(hid[cur.par][:, 0, 2 * i:2 * i + 2, :],
                                       bank[4 + 2 * cur.par + i][:, :].rearrange("p (c t) -> p c t", c=2),
                                       ACT.Relu).then_inc(b_hhi, 1)
            run_phase_b(act, step_b)
            normalise(Pair(None, GRID - 1, 4))

            def store_c(q):
                wait(act, c_sum, 1, q, 1)
                for dst, src in ((out[bass.ds(q.number * 2, 1), 0:PAT, :], o2[q.par][0:PAT, 0, :]),
                                 (out[bass.ds(q.number * 2 + 1, 1), 0:PAT, :], o2[q.par][PAT:P, 0, :]),
                                 (out[bass.ds(q.number * 2, 1), PAT:SEQ, :], o2[q.par][:, 1, :]),
                                 (out[bass.ds(q.number * 2 + 1, 1), PAT:SEQ, :], o2[q.par][:, 2, :])):
                    act.dma_start(dst.rearrange("a t d -> (a t) d"), src).then_inc(c_out[q.par], 16)

            run_phase_c(act, store_c)
            for i in range(2):
                act.wait_ge(c_out[i], 16 * 4 * (PAIRS // 2))

        @block.tensor
        def _(pe):
            pe.wait_ge(const_made, CONSTS)
            pe.wait_ge(noise_row, 1)
            for w in range(2):
                for c in range(2):
                    last = pe.matmul(bank[0][:, (2 * c + w) * P:(2 * c + w + 1) * P],
                                     nrow2[:, 0, (2 * w + c) * P:(2 * w + c + 1) * P],
                                     nrow2[:, 0, 512 + w * P:512 + (w + 1) * P], start=True, stop=True)
            last.then_inc(noise_outer, 1)
            pe.wait_ge(noise_done, 1)
            pe.wait_ge(wa_in, 128)

            def scores(pb, part):
                k, q = kst[pb.par], qst[pb.par]
                for n in range(3 * part, 3 * part + 3):
                    half, js = unit(n)
                    rows = slice(64 * half, 64 * half + STACK)
                    free, last_read = (pb, n - 2) if n >= 3 else (pb.back(1), n + 10)
                    wait(pe, a_exp, UNITS, free, last_read, settled if len(js) == 2 else None)
                    s = bank[5 + n % 3]
                    for at, j in enumerate(js):
                        for b in range(2):
                            queries = q[rows, j, b * SEQ:(b + 1) * SEQ]
                            if len(js) == 1:
                                dst, keys = s[:, b * SEQ:(b + 1) * SEQ], k[rows, j, PAT + b * TXT:PAT + (b + 1) * TXT]
                            else:
                                dst = s[PAT * b:PAT * (b + 1), at * SEQ:(at + 1) * SEQ]
                                keys = k[rows, j, b * (COLS - PAT):b * (COLS - PAT) + PAT]
                            last = pe.matmul(dst, keys, queries, start=True, stop=True)
                    last.then_inc(pe_s, 1)

            def weigh(pb, j):
                first_unit = 6 * (j // 2)
                wait(pe, a_exp, UNITS, pb, first_unit + (6 if j % 2 else 4))
                if j % 2 == 0:
                    if j:
                        wait(pe, a_cx, 2, pb, 1)
                    else:
                        wait(pe, a_cx, 2, pb.back(1), 2)
                v = vx[pb.par]
                for b in range(2):
                    for part in range(2):
                        for half in range(2):
                            hd = 2 * j + half
                            q4 = 32 * (hd % 4)
                            dst = bank[2][q4:q4 + 32, b * SEQ:(b + 1) * SEQ]
                            if part == 0:
                                text = pex[first_unit + 4 * (j % 2) + half]
                                pe.matmul(dst, v[:, 1 + b, hd, :], text[:, b * SEQ:(b + 1) * SEQ], start=True, stop=False)
                            else:
                                patch = pex[first_unit + 2 + half]
                                last = pe.matmul(dst, v[:, 3 * b, hd, :], patch[:, (j % 2) * SEQ:(j % 2 + 1) * SEQ],
                                                 start=False, stop=True)
                last.then_inc(pe_av, 1)

            def maxima(pa, part):
                k, q = kst[pa.par], qst[pa.par]
                for n in range(3 * part, 3 * part + 3):
                    half, js = unit(n)
                    rows = slice(64 * half, 64 * half + STACK - 1)
                    free, last_read = (pa, n - 1) if n >= 2 else (pa.back(1), n + 11)
                    wait(pe, v_m, UNITS, free, last_read, settled if len(js) == 2 else None)
                    m = bank[3 + n % 2]
                    for at, j in enumerate(js):
                        for b in range(2):
                            keys = k[rows, j, b * SEQ:(b + 1) * SEQ]
                            if len(js) == 1:
                                dst, queries = m[:, b * SEQ:(b + 1) * SEQ], q[rows, j, PAT + b * TXT:PAT + (b + 1) * TXT]
                            else:
                                dst = m[PAT * b:PAT * (b + 1), at * SEQ:(at + 1) * SEQ]
                                queries = q[rows, j, b * (COLS - PAT):b * (COLS - PAT) + PAT]
                            last = pe.matmul(dst, queries, keys, start=True, stop=True)
                    last.then_inc(pe_m, 1)

            def step(pa, pb, pc, has_a, has_b, has_c):
                if has_a:
                    wait_dma(pe, xin_in, 1, pa)
                    wait(pe, v_y, 1, pa.back(2), 1)
                    for w in range(2):
                        for c in range(2):
                            last = pe.matmul(bank[0][:, w * P:(w + 1) * P], w12[:, c, w, :], xin[pa.par][:, c, :],
                                             start=(c == 0), stop=(c == 1))
                    last.then_inc(pe_tok, 1)
                if has_a:
                    wait(pe, v_ga, 1, pa, 1)
                    wait(pe, v_mxt, 1, pa.back(1), 1)
                    pe.matmul(bank[1][:, 0:P], ga[:, :], w3[:, :], start=True, stop=True).then_inc(pe_w3, 1)
                if has_b:
                    wait_dma(pe, max_in, 8, pb)
                    wait(pe, a_v, 1, pb, 1)
                    scores(pb, 0)
                if has_a:
                    wait(pe, a_xn, 3, pa, 3)
                    wait(pe, v_h, 1, pa, 1)
                    for k in range(TILES):
                        last = pe.transpose(bank[1][:, k * P:(k + 1) * P], xn[pa.par][:, k, :], ident[:, :])
                    last.then_inc(pe_tr, 1)
                if has_a:
                    wait(pe, a_xt, 1, pa, 1)
                    for i in range(2):
                        pe.matmul(halves(bank[i][:, 0:COLS], PAT), wqkv[:, i, :], xT[:, 0:P], start=True, stop=True)
                        pe.matmul(bank[i][:, PAT:PAT + 2 * TXT], wqkv[:, i, :], xT[:, P:COLS], start=True,
                                  stop=True).then_inc(pe_qk, 1)
                if has_b:
                    scores(pb, 1)
                if has_a:
                    wait(pe, v_qklo, 1, pa, 1)
                    for k in range(TILES):
                        last = pe.matmul(bank[1][:, k * P:(k + 1) * P], xT[:, k * P:(k + 1) * P], wqkv[:, 2, :],
                                         start=True, stop=True)
                    last.then_inc(pe_v, 1)
                if has_c:
                    wait(pe, a_x2, 3, pc, 3)
                    if has_a:
                        wait(pe, v_qklo, 1, pa, 1)
                    if pc.loop is None and pc.off >= PAIRS - 2:
                        wait(pe, v_y, 1, pc, 1)
                        if has_b:
                            wait(pe, v_y, 1, pb.back(1), 1)
                    for k in range(TILES):
                        last = pe.transpose(bank[0][:, k * P:(k + 1) * P], pay[pc.par][:, k, 0:D], ident[:, :])
                    last.then_inc(pe_x2tr, 1)
                if has_b:
                    weigh(pb, 0)
                    scores(pb, 2)
                if has_c:
                    wait(pe, a_x2t, 1, pc, 1)
                    if has_a:
                        wait(pe, v_qklo, 1, pa, 1)
                    for k in range(TILES):
                        last = pe.matmul(bank[0][:, k * NE:(k + 1) * NE], x2T[:, k * P:(k + 1) * P], rw[:, :],
                                         start=True, stop=True)
                    last.then_inc(pe_log, 1)
                if has_b:
                    weigh(pb, 1)
                if has_b:
                    scores(pb, 3)
                if has_a:
                    wait_dma(pe, st_in, 4, pa)
                    maxima(pa, 0)
                if has_b:
                    weigh(pb, 2)
                if has_a:
                    maxima(pa, 1)
                if has_c:
                    wait(pe, v_oh, 1, pc, 1)
                    wait(pe, v_lg, 1, pc, 1)
                    for k in range(TILES):
                        for i in range(k + 1):
                            pe.matmul(bank[0][:, k * NE:(k + 1) * NE], before[:, :] if i == k else onesb[:, :],
                                      ohs[:, i, :], start=(i == 0), stop=(i == k))
                    for i in range(TILES):
                        last = pe.matmul(bank[0][:, TILES * NE:(TILES + 1) * NE], onesb[:, :], ohs[:, i, :],
                                         start=(i == 0), stop=(i == TILES - 1))
                    last.then_inc(pe_rank, 1)
                if has_b:
                    weigh(pb, 3)
                    if has_a:
                        wait(pe, a_v, 1, pa, 1)
                    wait(pe, a_cx, 2, pb, 2)
                    for k in (1, 2, 0):
                        if k == 0:
                            if has_c:
                                wait(pe, v_rank, 1, pc, 1)
                        for g in range(2):
                            dst = bank[1][:, (2 * (k - 1) + g) * P:(2 * (k - 1) + g + 1) * P] if k else \
                                bank[0][:, g * P:(g + 1) * P]
                            last = pe.transpose(dst, cx[g][:, k * P:(k + 1) * P], ident[:, :])
                        if k != 1:
                            last.then_inc(pe_ctr, 1)
                if has_a:
                    maxima(pa, 2)
                if has_b:
                    wait(pe, v_cn, 1, pb, 1)
                    for k in range(TILES):
                        last = pe.transpose(bank[1][:, k * P:(k + 1) * P], cn[:, k, :], ident[:, :])
                    last.then_inc(pe_cnt, 1)
                if has_a:
                    maxima(pa, 3)
                    wait(pe, v_m, UNITS, pa, UNITS)
                    if has_b:
                        wait(pe, a_ct, 1, pb, 1)
                    else:
                        wait(pe, a_v, 1, pa, 1)
                    for k in range(TILES):
                        last = pe.transpose(tile_cols(bank[1][0:HEADS, 0:COLS], k),
                                            mx[:, k, :, :].rearrange("p a b -> p (a b)"), ident[:, :])
                    last.then_inc(pe_mxt, 1)
                if has_b:
                    wait(pe, a_ct, 1, pb, 1)
                    for k in range(TILES):
                        last = pe.matmul(bank[0][:, k * P:(k + 1) * P], cT[:, k * P:(k + 1) * P], wo[:, :],
                                         start=True, stop=True)
                    last.then_inc(pe_o, 1)

            run_phase_a(pe, step)

            ones2 = ones16x[0:2, :]

            def step_b(nxt, cur, old, has_nxt, has_cur, has_old):
                if has_nxt:
                    wait_dma(pe, xs_in, 1, nxt, 4)
                    wait(pe, b_xlo, 1, nxt.back(2), 1)
                    for k in range(2):
                        last = pe.transpose(bank[nxt.par][:, k * P:(k + 1) * P], xs[nxt.slot][:, k, 0:D], ident[:, :])
                    last.then_inc(b_xt, 1)
                if has_cur:
                    wait_dma(pe, w1_in, 1, cur, 4)
                    wait_dma(pe, bs_in, 1, cur, 4)
                    wait(pe, b_xlo, 1, cur, 1)
                    wait(pe, b_xhi, 1, cur, 1)
                    w, x = w1s[cur.slot], xsT[cur.par]
                    for i in range(2):
                        wait(pe, b_hlo, 2, cur.back(2), i + 1)
                        dst = bank[4 + 2 * cur.par + i]
                        for c in range(2):
                            f = (2 * i + c) * P
                            o = dst[:, c * G:(c + 1) * G]
                            pe.matmul(o, w[:, 0, f:f + P], x[:, 0, :], start=True, stop=False)
                            pe.matmul(o, w[:, 0, f:f + P], x[:, 1, :], start=False, stop=False)
                            pe.matmul(o, w[:, 1, f:f + P], x[:, 0, :], start=False, stop=False)
                            last = pe.matmul(o, bs[cur.slot][:, f:f + P], ones2[:, :], start=False, stop=True)
                        last.then_inc(b_up, 1)
                if has_old:
                    wait_dma(pe, w2_in, 1, old, 4)
                    wait(pe, b_z, 1, old.back(2), 1)
                    wait(pe, b_hhi, 2, old, 2)
                    wait(pe, b_hlo, 2, old, 2)
                    w = w2s[old.slot][:, 0:2 * F].rearrange("p (s c d) -> p s c d", s=2, c=FC)
                    hh = hid[old.par]
                    for k in range(2):
                        o = bank[2 + old.par][:, k * D:(k + 1) * D]
                        pe.matmul(o, ones2[:, 0:P], bs[old.slot][:, F:F + D], start=True, stop=False)
                        for c in range(FC):
                            pe.matmul(o, hh[:, 0, c, k * P:(k + 1) * P], w[:, 0, c, :], start=False, stop=False)
                            pe.matmul(o, hh[:, 0, c, k * P:(k + 1) * P], w[:, 1, c, :], start=False, stop=False)
                            last = pe.matmul(o, hh[:, 1, c, k * P:(k + 1) * P], w[:, 0, c, :], start=False,
                                             stop=(c == FC - 1))
                    last.then_inc(b_dn, 1)

            run_phase_b(pe, step_b)

        @block.vector
        def _(dve):
            for i in range(2):
                dve.memset(kst[i][32:64, :, :], MAXROW)
                dve.memset(kst[i][96:128, :, :], MAXROW)
                dve.memset(vx[i][PAT:P, 0, :, :], 0.0)
                dve.memset(vx[i][0:PAT, 3, :, :], 0.0)
                dve.memset(vx[i][0:PAT, 0, :, HD:2 * HD], 1.0)
                dve.memset(vx[i][:, 1:3, :, HD:2 * HD], 1.0)
                dve.memset(vx[i][PAT:P, 3, :, HD:2 * HD], 1.0).then_inc(const_made, 1)
            prep = Chain(dve, dve_prep, 6, Pair(None, 0))
            dve.wait_ge(w_in, 64)
            dve.wait_ge(noise_root, 4)
            dve.tensor_scalar(nrow2[:, 0, :], nrow[:, :], 0.0, None, ALU.is_lt)
            prep(dve.tensor_scalar(ncol2[:, 2:4], ncol[:, 4:6], 0.0, None, ALU.is_lt))
            dve.tensor_scalar(nrow2[:, 0, :], nrow2[:, 0, :], -2.0, 1.0, ALU.mult, ALU.add)
            prep(dve.tensor_scalar(ncol2[:, 2:4], ncol2[:, 2:4], -2.0, 1.0, ALU.mult, ALU.add))
            dve.tensor_tensor(nrow2[:, 0, :], nrow2[:, 0, :], nrow2[:, 1, :], ALU.mult).then_inc(noise_row, 1)
            prep(dve.tensor_tensor(ncol2[:, 0:2], ncol2[:, 0:2], ncol2[:, 2:4], ALU.mult))
            prep(dve.tensor_tensor(ncol2[:, 0:2], ncol2[:, 0:2], ncol[:, 2:4], ALU.mult))
            prep(dve.tensor_tensor(ncol2[:, 0:2], ncol2[:, 0:2], ncol[:, 0:2], ALU.add))
            dve.wait_ge(noise_outer, 1)
            prep(dve.tensor_tensor(sw12[:, :, :, :].rearrange("p a b c -> p (a b c)"),
                                   sw12[:, :, :, :].rearrange("p a b c -> p (a b c)"), bank[0][:, :], ALU.mult))
            prep.end()
            dve.wait_ge(wa_in, 128)
            dve.tensor_tensor(posb[:, :], posb[:, :], b3r[:, :], ALU.add)
            dve.tensor_tensor(w12[:, :, :, :].rearrange("p a b c -> p (a b c)"), w12[:, :, :, :]
                              .rearrange("p a b c -> p (a b c)"), sw12[:, :, :, :]
                              .rearrange("p a b c -> p (a b c)"), ALU.add).then_inc(noise_done, 1)
            dve.wait_ge(noise_done, 1)
            dve.wait_ge(const_made, CONSTS)

            def norm_stats(link, x, stat, mv, ve, eps, n, done, wait_free):
                for k in range(n):
                    ins = dve.bn_stats(stat[:, k, :], x(k))
                link(ins, settled)
                for k in range(n):
                    ins = dve.bn_aggr(mv[:, k, :], stat[:, k, :])
                link(ins)
                wait_free()
                dve.tensor_scalar(ve[:, 0, :], mv[:, :, 1], eps, None, ALU.add)
                dve.tensor_scalar(ve[:, 1, :], mv[:, :, 0], -1.0, None, ALU.mult).then_inc(done, 1)

            def reduce_max(pa, part):
                for n in range(3 * part, 3 * part + 3):
                    half, js = unit(n)
                    wait(dve, pe_m, UNITS, pa, n + 1)
                    if n == 0:
                        wait(dve, pe_mxt, 1, pa.back(1), 1)
                    dst = mx[:, 1:TILES, half, js[0]] if len(js) == 1 else mx[:, 0, half, js[0]:js[0] + 2]
                    dve.tensor_reduce(dst, bank[3 + n % 2][:, 0:COLS].rearrange("p (c s) -> p c s", c=2),
                                      AX.X, ALU.max).then_inc(v_m, 1)

            def step(pa, pb, pc, has_a, has_b, has_c):
                if has_a:
                    c1 = Chain(dve, chain1, 7, pa)
                    wait(dve, pe_tok, 1, pa, 1)
                    wait(dve, a_exp_g, 1, pa.back(1), 1)
                    dve.tensor_scalar(gm[:, :], bank[0][:, 0:P], ncol2[:, 0:1], 20.0, ALU.add, ALU.min).then_inc(v_gm, 1)
                if has_a:
                    wait(dve, a_exp_g, 1, pa, 1)
                    c1(dve.scalar_tensor_tensor(out=gn[:, :], in0=ge[:, :], scalar=2.0, in1=ge[:, :], op0=ALU.add,
                                                op1=ALU.mult))
                    c1(dve.tensor_scalar(gg[:, :], gn[:, :], 2.0, None, ALU.add))
                    c1(dve.reciprocal(gr[:, :], gg[:, :]))
                    c1(dve.tensor_tensor(gt[:, :], gn[:, :], gr[:, :], ALU.mult))
                    c1(dve.scalar_tensor_tensor(out=gg[:, :], in0=bank[0][:, 0:P], scalar=ncol2[:, 0:1], in1=gt[:, :],
                                                op0=ALU.add, op1=ALU.mult))
                    wait(dve, pe_w3, 1, pa.back(1), 1)
                    dve.scalar_tensor_tensor(out=ga[:, :], in0=bank[0][:, P:2 * P], scalar=ncol2[:, 1:2], in1=gg[:, :],
                                             op0=ALU.add, op1=ALU.mult).then_inc(v_ga, 1)
                    wait(dve, pe_w3, 1, pa, 1)
                    wait(dve, p_kept, 1, pa.back(4), 1)
                    dve.tensor_tensor(h[pa.slot][:, 0, :], bank[1][:, 0:P], posb[:, :], ALU.add).then_inc(v_h, 1)
                    wait(dve, v_h, 1, pa, 1)
                    wait_dma(dve, txt_in, 2, pa)
                    norm_stats(c1, lambda k: h[pa.slot][:, k, :], stat1, mv1, ve1, EPS_LN, TILES, v_st1,
                               lambda: wait(dve, p_st1, 2, pa.back(1), 2))
                if has_c:
                    c3 = Chain(dve, chain3, 11, pc)
                    wait(dve, p_kept, 1, pc, 1)
                    norm_stats(c3, lambda k: kept[pc.par][:, k, 0:D], stat3, mv3, ve3, EPS_LN, TILES,
                               v_st3, lambda: wait(dve, p_st3, 2, pc.back(1), 2))
                if has_a:
                    wait(dve, a_qkhi, 2, pa, 1)
                    wait_dma(dve, kq_out, 2, pa.back(1))
                    dve.tensor_tensor(kq[:, 2, :], bank[0][:, 0:COLS], kq[:, 3, :], ALU.subtract)
                    wait(dve, a_qkhi, 2, pa, 2)
                    dve.tensor_tensor(kq[:, 1, :], bank[1][:, 0:COLS], kq[:, 0, :], ALU.subtract).then_inc(v_qklo, 1)
                    c1.end()
                if has_c:
                    wait(dve, pe_log, 1, pc, 1)
                    dve.tensor_copy(lg[:, :, :], bank[0][:, 0:TILES * NE].rearrange("p (t e) -> p t e", t=TILES)).then_inc(v_lg, 1)
                    wait(dve, v_lg, 1, pc, 1, settled)
                    for k in range(TILES):
                        ins = dve.max(top[:, k, :], lg[:, k, :])
                    c3(ins)
                    wait(dve, a_gex, 1, pc.back(1), 1)
                    dve.tensor_tensor(gap[:, :], top[:, :, 1], top[:, :, 0], ALU.subtract).then_inc(v_gap, 1)
                    for k in range(TILES):
                        ins = dve.max_index(topi[:, k, :], top[:, k, :], lg[:, k, :])
                    c3(ins)
                    c3(dve.tensor_copy(topf[:, :, :], topi[:, :, 0:2]))
                    i8 = iota8[:, :].unsqueeze(1).to_broadcast([P, TILES, NE])
                    dve.tensor_tensor(oh1[:, :, :], i8, topf[:, :, 0:1].to_broadcast([P, TILES, NE]), ALU.is_equal)
                    c3(dve.tensor_tensor(oh2[:, :, :], i8, topf[:, :, 1:2].to_broadcast([P, TILES, NE]), ALU.is_equal))
                    wait(dve, pe_rank, 1, pc.back(1), 1)
                    dve.tensor_tensor(ohs[:, :, :], oh1[:, :, :], oh2[:, :, :], ALU.add).then_inc(v_oh, 1)
                    wait_dma(dve, sent, 6, pc.back(2))
                    dve.tensor_copy(pay[pc.par][:, :, D], tok[:, :])
                    dve.tensor_copy(pay[pc.par][:, :, D + 1], topf[:, :, 0])
                    wait(dve, a_gex, 1, pc, 1)
                    wait_dma(dve, kept_out, 1, pc.back(2))
                    c3(dve.tensor_scalar(gsum[:, :], gex[:, :], 1.0, None, ALU.add))
                    c3(dve.reciprocal(kept[pc.par][:, :, D], gsum[:, :]))
                    dve.tensor_tensor(kept[pc.par][:, :, D + 1], gex[:, :], kept[pc.par][:, :, D], ALU.mult).then_inc(v_gate, 1)
                    dve.tensor_scalar(tok[:, :], tok[:, :], float(COLS), None, ALU.add)
                if has_a:
                    reduce_max(pa, 0)
                    reduce_max(pa, 1)
                if has_c:
                    wait(dve, pe_rank, 1, pc, 1)
                    c3(dve.tensor_tensor(rank[:, :, :], bank[0][:, 0:TILES * NE].rearrange("p (t e) -> p t e", t=TILES),
                                         base[:, :].unsqueeze(1).to_broadcast([P, TILES, NE]), ALU.add))
                    dve.tensor_tensor(base[:, :], base[:, :], bank[0][:, TILES * NE:(TILES + 1) * NE], ALU.add).then_inc(v_rank, 1)
                    dve.tensor_tensor(sl1[:, :, :], oh1[:, :, :], rank[:, :, :], ALU.mult)
                    c3(dve.tensor_tensor(sl2[:, :, :], oh2[:, :, :], rank[:, :, :], ALU.mult))
                    dve.tensor_reduce(slf[:, 0, :], sl1[:, :, :], AX.X, ALU.add)
                    c3(dve.tensor_reduce(slf[:, 1, :], sl2[:, :, :], AX.X, ALU.add))
                    dve.tensor_copy(slot[pc.par][:, :, :], slf[:, :, :]).then_inc(v_slot, 1)
                    c3.end()
                if has_b:
                    c2 = Chain(dve, chain2, 3, pb)
                    wait(dve, pe_ctr, 2, pb, 2)
                    views = []
                    for k in range(TILES):
                        t = bank[0][:, 0:2 * P] if k == 0 else bank[1][:, (k - 1) * 2 * P:k * 2 * P]
                        views.append(t.rearrange("p (h r) -> p h r", h=HEADS))
                    for k in range(TILES):
                        ins = dve.reciprocal(rden[:, k, :], views[k][:, :, HD])
                    c2(ins)
                    wait(dve, pe_cnt, 1, pb.back(1), 1)
                    for k in range(TILES):
                        ins = dve.tensor_tensor(cn[:, k, :].rearrange("p (h r) -> p h r", h=HEADS), views[k][:, :, 0:HD],
                                                rden[:, k, :].unsqueeze(2).to_broadcast([P, HEADS, HD]), ALU.mult)
                    ins.then_inc(v_cn, 1)
                if has_a:
                    reduce_max(pa, 2)
                    reduce_max(pa, 3)
                    wait(dve, pe_mxt, 1, pa, 1)
                    wait_dma(dve, max_in, 8, pa.back(1))
                    dve.tensor_scalar(mxT[:, :], bank[1][0:HEADS, 0:COLS], -1.0 / MAXROW, None, ALU.mult).then_inc(v_mxt, 1)
                if has_b:
                    wait(dve, pe_o, 1, pb, 1)
                    wait(dve, a_yn, 3, pb.back(1), 3)
                    ins = dve.tensor_tensor(y[:, :, :].rearrange("p t d -> p (t d)"), bank[0][:, 0:COLS],
                                            xn[pb.par][:, :, :].rearrange("p t d -> p (t d)"), ALU.add)
                    ins.then_inc(v_y, 1)
                    wait(dve, v_y, 1, pb, 1)
                    norm_stats(c2, lambda k: y[:, k, :], stat2, mv2, ve2, EPS_ATT, TILES, v_st2,
                               lambda: wait(dve, p_st2, 2, pb.back(1), 2))
                    c2.end()

            run_phase_a(dve, step)

            link = Chain(dve, chain5, 12, Pair(None, 0))
            wait(dve, v_rank, 1, Pair(None, PAIRS - 1), 1)
            link(dve.tensor_tensor(cnt[:, :], base[:, :], ecap[:, :], ALU.subtract))
            link(dve.tensor_scalar(cnti[:, :], cnt[:, :], float(G - 1), None, ALU.add))
            link(dve.tensor_scalar(cntt[:, :], cnti[:, :], G.bit_length() - 1, None, ALU.arith_shift_right))
            link(dve.tensor_copy(ntl[:, :], cntt[:, :]))
            link(dve.tensor_tensor_scan(cum[:, :], one8[:, :], ntl[:, :], 0.0, ALU.mult, ALU.add))
            link(dve.tensor_tensor(past[:, :, :], iotag[:, :].unsqueeze(2).to_broadcast([P, GRID, NE]),
                                   cum[:, :].unsqueeze(1).to_broadcast([P, GRID, NE]), ALU.is_ge))
            dve.tensor_reduce(eg[:, :], past[:, :, :], AX.X, ALU.add)
            link(dve.tensor_tensor(pastn[:, :, :], past[:, :, :], ntl[:, :].unsqueeze(1).to_broadcast([P, GRID, NE]), ALU.mult))
            link(dve.tensor_reduce(cg[:, :], pastn[:, :, :], AX.X, ALU.add))
            link(dve.tensor_tensor(rg[:, :], iotag[:, :], cg[:, :], ALU.subtract))
            link(dve.tensor_scalar(rg2[:, :], rg[:, :], float(G), None, ALU.mult))
            link(dve.scalar_tensor_tensor(out=rg[:, :], in0=eg[:, :], scalar=float(CAP), in1=rg2[:, :], op0=ALU.mult, op1=ALU.add))
            dve.tensor_scalar(plan[:, 0, :], rg[:, :], float(NE * CAP), None, ALU.min)
            dve.tensor_scalar(plan[:, 1, :], eg[:, :], float(NE - 1), None, ALU.min)
            dve.tensor_scalar(padf[:, 0, :], base[:, :], lane[:, 0:1], None, ALU.add)
            link(dve.tensor_scalar(padf[:, 1, :], base[:, :], lane[:, 1:2], None, ALU.add))
            dve.tensor_copy(padi[:, :, :], padf[:, :, :]).then_inc(plan_made, 1)
            link.end()

            def step_b(nxt, cur, old, has_nxt, has_cur, has_old):
                if has_nxt:
                    wait(dve, b_xhi, 1, nxt, 1)
                    wait(dve, b_up, 2, nxt.back(2), 2)
                    dve.tensor_tensor(xsT[nxt.par][:, 1, :], bank[nxt.par][:, 0:G], xsT[nxt.par][:, 0, :],
                                      ALU.subtract).then_inc(b_xlo, 1)
                if has_old:
                    link = Chain(dve, chain4, 3, old)
                    wait(dve, b_dn, 1, old, 1)
                    wait(dve, b_zn, 2, old.back(2), 2)
                    dve.tensor_tensor(z[old.par][:, :, :], bank[2 + old.par][:, 0:2 * D].rearrange("p (c d) -> p c d", c=2),
                                      xs[old.slot][:, :, 0:D], ALU.add).then_inc(b_z, 1)
                    wait_dma(dve, w2_in, 1, old, 4)
                    link(dve.tensor_scalar(first[:, :], xs[old.slot][:, :, D + 1],
                                           w2s[old.slot][:, WROW2 - 2:WROW2].bitcast(F32), None, ALU.is_equal))
                    wait_dma(dve, ye_out, 2, old.back(4))
                    dve.scalar_tensor_tensor(out=dest[old.slot][:, :], in0=first[:, :], scalar=-float(TOKENS),
                                             in1=xs[old.slot][:, :, D], op0=ALU.mult, op1=ALU.add).then_inc(b_dest, 1)
                if has_cur:
                    for i in range(2):
                        wait(dve, b_hhi, 2, cur, i + 1)
                        dve.scalar_tensor_tensor(out=hid[cur.par][:, 1, 2 * i:2 * i + 2, :].rearrange("p c t -> p (c t)"),
                                                 in0=bank[4 + 2 * cur.par + i][:, :], scalar=0.0,
                                                 in1=hid[cur.par][:, 0, 2 * i:2 * i + 2, :].rearrange("p c t -> p (c t)"),
                                                 op0=ALU.max, op1=ALU.subtract).then_inc(b_hlo, 1)
                        if has_old and i == 0:
                            for k in range(2):
                                ins = dve.bn_stats(stat4[:, k, :], z[old.par][:, k, :])
                            link(ins, settled)
                            for k in range(2):
                                ins = dve.bn_aggr(mv4[:, k, :], stat4[:, k, :])
                            link(ins)
                elif has_old:
                    for k in range(2):
                        ins = dve.bn_stats(stat4[:, k, :], z[old.par][:, k, :])
                    link(ins)
                    for k in range(2):
                        ins = dve.bn_aggr(mv4[:, k, :], stat4[:, k, :])
                    link(ins)
                if has_old:
                    wait(dve, p_st4, 2, old.back(1), 2)
                    dve.tensor_scalar(ve4[:, 0, :], mv4[:, :, 1], EPS_FFN, None, ALU.add)
                    dve.tensor_scalar(ve4[:, 1, :], mv4[:, :, 0], -1.0, None, ALU.mult).then_inc(b_st, 1)
                    link.end()

            run_phase_b(dve, step_b)

            def combine(q):
                wait(dve, c_sum, 1, q.back(2), 1)
                wait_dma(dve, c_in, 3, q)
                for k in range(TILES):
                    ins = dve.scalar_tensor_tensor(out=o1[q.par][:, k, :], in0=y1[q.par][:, k, :], scalar=kc[q.par][:, k, D:D + 1],
                                                   in1=kc[q.par][:, k, 0:D], op0=ALU.mult, op1=ALU.add)
                ins.then_inc(c_chain, 1)
                wait(dve, c_chain, 1, q, 1)
                wait_dma(dve, c_out, 4, q.back(2))
                for k in range(TILES):
                    ins = dve.scalar_tensor_tensor(out=o2[q.par][:, k, :], in0=y2[q.par][:, k, :],
                                                   scalar=kc[q.par][:, k, D + 1:D + 2], in1=o1[q.par][:, k, :],
                                                   op0=ALU.mult, op1=ALU.add)
                ins.then_inc(c_sum, 1)

            run_phase_c(dve, combine)

        @block.gpsimd
        def _(pool):
            pool.memset(ident[:, :], 0.0).then_inc(pool_prep, 1)
            pool.memset(before[:, :], 1.0).then_inc(pool_prep, 1)
            pool.wait_ge(pool_prep, 2)
            pool.affine_select(out=ident[:, :], in_=ident[:, :], compare_op=ALU.not_equal, fill=1.0, base=0,
                               pattern=[[-1, P]], channel_multiplier=1).then_inc(const_made, 1)
            pool.affine_select(out=before[:, :], in_=before[:, :], compare_op=ALU.is_gt, fill=0.0, base=0,
                               pattern=[[1, P]], channel_multiplier=-1).then_inc(const_made, 1)
            pool.memset(onesb[:, :], 1.0).then_inc(const_made, 1)
            pool.memset(ones16x[:, :], 1.0).then_inc(const_made, 1)
            pool.iota(iota8[:, :], [[1, NE]], base=0, channel_multiplier=0, allow_small_or_imprecise_dtypes=True).then_inc(const_made, 1)
            pool.iota(ecap[:, :], [[CAP, NE]], base=0, channel_multiplier=0, allow_small_or_imprecise_dtypes=True).then_inc(const_made, 1)
            pool.iota(base[:, :], [[CAP, NE]], base=0, channel_multiplier=0, allow_small_or_imprecise_dtypes=True).then_inc(const_made, 1)
            pool.iota(tok[:, :], [[P, TILES]], base=TOKENS, channel_multiplier=1, allow_small_or_imprecise_dtypes=True)
            pool.iota(iotag[:, :], [[1, GRID]], base=0, channel_multiplier=0, allow_small_or_imprecise_dtypes=True)
            pool.iota(lane[:, :], [[P, 2]], base=0, channel_multiplier=1, allow_small_or_imprecise_dtypes=True)
            pool.memset(one8[:, :], 1.0)
            pool.memset(expert[:, :], 0.0)
            pool.memset(neghalf[:, :], -0.5)
            for i in range(2):
                pool.memset(pay[i][:, :, D + 2:ROW], 0.0)
            pool.memset(padrow[:, 0:D], 0.0)
            pool.memset(padrow[:, D + 1:ROW], 0.0)
            pool.memset(padrow[:, D:D + 1], FAR).then_inc(const_made, 2)
            pool.wait_ge(const_made, CONSTS)
            for i in range(2):
                pool.dma_start(sorted_d[NE * CAP + i * P:NE * CAP + (i + 1) * P, :], padrow[:, :]).then_inc(pads_sent, 16)

            for r in range(2):
                view = bstage[32 * r:32 * r + 1, :].rearrange("p (e c) -> p e c", e=NE)
                pool.dma_start(view[:, :, 0:F], a["b1"].unsqueeze(0)).then_inc(bstage_in, 16)
                pool.dma_start(view[:, :, F:F + D], a["b2"].unsqueeze(0)).then_inc(bstage_in, 16)
            pool.wait_ge(bstage_in, 64)
            for r in range(2):
                pool.tensor_copy(bsplit[32 * r:32 * r + 1, :], bstage[32 * r:32 * r + 1, :]).then_inc(bhi_made, 1)
            pool.wait_ge(bhi_made, 2)
            pool.tensor_tensor(bsplit[32:33, :], bstage[32:33, :], bsplit[32:33, :], ALU.subtract).then_inc(bsplit_made, 1)
            pool.wait_ge(bsplit_made, 1)
            for r in range(2):
                pool.dma_start(bias_d[:, r, :].unsqueeze(0), bsplit[32 * r:32 * r + 1, :].rearrange("p (e c) -> p e c", e=NE)
                               ).then_inc(bsplit_out, 16)
            def split_weights(q):
                wait_dma(pool, stage_in, 3 if q.par else 1, q, 2, settled)
                wait_dma(pool, split_out, 1, q.back(2), 2, settled)
                dst = split2 if q.par else split1
                src = stage[q.par]
                if q.par:
                    pool.tensor_copy(dst[:, WROW2 - 2:WROW2].bitcast(F32), expert[:, :])
                pool.tensor_copy(dst[:, 0:F], src[:, :]).then_inc(split_made, 1)
                wait(pool, split_made, 2, q, 1)
                last = pool.tensor_tensor(dst[:, F:2 * F], src[:, :], dst[:, 0:F], ALU.subtract)
                if q.par:
                    last = pool.tensor_scalar(expert[:, :], expert[:, :], 1.0, None, ALU.add)
                last.then_inc(split_made, 1)

            def scale_shift(made, per, item, ve, rs, nm, n, done, used):
                wait(pool, made, per, item, per)
                used()
                pool.tensor_tensor(rs, ve[:, 0, :], neghalf[:, 0:n], ALU.pow).then_inc(done, 1)
                wait(pool, done, 2, item, 1)
                pool.tensor_tensor(nm, ve[:, 1, :], rs, ALU.mult).then_inc(done, 1)

            def step(pa, pb, pc, has_a, has_b, has_c):
                if has_a:
                    scale_shift(v_st1, 1, pa, ve1, rs1[:, :], nm1[:, :], TILES, p_st1,
                                lambda: wait(pool, a_xn, 3, pa.back(1), 3))
                if has_c:
                    scale_shift(v_st3, 1, pc, ve3, rs3[:, :], nm3[:, :], TILES, p_st3,
                                lambda: wait(pool, a_x2, 3, pc.back(1), 3))
                if has_a:
                    split_weights(pa)
                if has_c:
                    wait(pool, v_slot, 1, pc, 1, settled)
                    for k in range(TILES):
                        for w in range(2):
                            pool.indirect_dma_start(
                                sorted_d[:, :], bass.IndirectOffsetOnAxis(ap=slot[pc.par][:, w, k:k + 1], axis=0),
                                pay[pc.par][:, k, :], None).then_inc(sent[pc.par], 16)
                if has_b:
                    scale_shift(v_st2, 1, pb, ve2, rs2[:, :], nm2[:, :], TILES, p_st2,
                                lambda: wait(pool, a_yn, 3, pb.back(1), 3))
                    wait(pool, a_yn, 3, pb, 3)
                    g3 = lng[:, :].unsqueeze(1).to_broadcast([P, TILES, D])
                    b3 = lnb[:, :].unsqueeze(1).to_broadcast([P, TILES, D])
                    pool.tensor_tensor(yg[:, :, :], yn[:, :, :], g3, ALU.mult).then_inc(p_yg, 1)
                    wait(pool, p_yg, 1, pb, 1)
                    pool.tensor_tensor(yg[:, :, :], yg[:, :, :], b3, ALU.add).then_inc(p_chain, 1)
                    wait(pool, p_chain, 1, pb, 1)
                    wait_dma(pool, kept_out, 1, pb.back(2))
                    pool.tensor_tensor(kept[pb.par][:, :, 0:D], yg[:, :, :], h[pb.slot][:, :, :], ALU.add).then_inc(p_kept, 1)

            run_phase_a(pool, step)

            pool.wait_ge(plan_made, 1)
            for e in range(NE):
                for i in range(2):
                    pool.indirect_dma_start(sorted_d[:, :], bass.IndirectOffsetOnAxis(ap=padi[:, i, e:e + 1], axis=0),
                                            padrow[:, :], None).then_inc(pads_sent, 16)

            def finish(q):
                gb = w2s[q.slot][:, 2 * F:2 * F + 4 * D].bitcast(F32)
                wait(pool, b_zn, 2, q, 2)
                pool.tensor_tensor(zg[:, :, :], zn[q.par][:, :, :], gb[:, 0:D].unsqueeze(1).to_broadcast([P, 2, D]),
                                   ALU.mult).then_inc(b_zg, 1)
                wait(pool, b_zg, 1, q, 1)
                wait_dma(pool, ye_out, 2, q.back(2))
                pool.tensor_tensor(ye[q.par][:, :, :], zg[:, :, :], gb[:, D:2 * D].unsqueeze(1).to_broadcast([P, 2, D]),
                                   ALU.add).then_inc(b_ye, 1)
                wait(pool, b_ye, 1, q, 1, settled)
                wait(pool, b_dest, 1, q, 1)
                for k in range(2):
                    pool.indirect_dma_start(expert_d[:, :], bass.IndirectOffsetOnAxis(ap=dest[q.slot][:, k:k + 1], axis=0),
                                            ye[q.par][:, k, :], None, bounds_check=2 * TOKENS - 1, oob_is_err=False
                                            ).then_inc(ye_out[q.par], 16)

            def step_b(nxt, cur, old, has_nxt, has_cur, has_old):
                before = old.back(1)
                if has_old:
                    scale_shift(b_st, 1, old, ve4, rs4b[old.par][:, :], nm4[old.par][:, :], 2, p_st4,
                                lambda: wait(pool, b_zn, 2, old.back(2), 2))
                if before.loop is not None or before.off >= 0:
                    finish(before)

            run_phase_b(pool, step_b)
            finish(Pair(None, GRID - 1, 4))


def kernel(**inputs):
    import numpy as _np
    import concourse.bacc as _bacc
    from concourse import mybir as _mybir
    from concourse.bass_utils import run_bass_kernel_spmd as _run

    i = {k.replace("L0_", ""): _np.asarray(v) for k, v in inputs.items()}
    xp = i["x"].reshape(PAIRS, 2, 8, 2, 8, 8, 16).transpose(0, 4, 6, 3, 1, 2, 5).reshape(PAIRS, P, 2, P)

    def both(u, v):
        return _np.stack([u.T.reshape(2, P, P), v.T.reshape(2, P, P)], axis=2).transpose(1, 0, 2, 3)

    def by_feature(w):
        return w.reshape(D, HEADS // 2, 2, HD).transpose(0, 3, 2, 1).reshape(D, D)

    at = _np.arange(PAT, dtype=_np.float32)[:, None] * _np.exp(
        _np.arange(0, D, 2, dtype=_np.float32) * _np.float32(-_np.log(10000.0) / D))
    table = _np.stack([_np.sin(at), _np.cos(at)], axis=-1).reshape(PAT, D)
    arrays = {
        "xp": xp, "txt": i["txt"],
        "w12": both(i["tok_W1_w"], i["tok_W2_w"]), "sw12": both(i["tok_W1_sw"], i["tok_W2_sw"]),
        "noise_rows": _np.concatenate([i["tok_eps_in1"], i["tok_eps_in2"], i["tok_eps_out1"], i["tok_eps_out2"]])[None, :],
        "noise_cols": _np.stack([i["tok_W1_b"], i["tok_W2_b"], i["tok_W1_sb"], i["tok_W2_sb"], i["tok_eps_out1"],
                                 i["tok_eps_out2"]], axis=1),
        "w3": i["tok_W3_w"].T, "b3": i["tok_W3_b"][None, :], "pos": _np.concatenate([table, table]),
        "wqkv": _np.stack([by_feature(i["attn_W_q"].T), by_feature(i["attn_W_k"].T), i["attn_W_v"].T], axis=1), "wo": i["attn_W_o"].T,
        "ln_gamma": i["attn_ln_gamma"][None, :], "ln_beta": i["attn_ln_beta"][None, :],
        "router": i["ffn_router_w"], "w1": i["ffn_w1"], "w2": i["ffn_w2"], "b1": i["ffn_b1"], "b2": i["ffn_b2"],
        "gamma": i["ffn_gamma"], "beta": i["ffn_beta"],
    }
    nc = _bacc.Bacc("TRN2", target_bir_lowering=False, num_devices=1)
    arrays = {f"in_{k}": _np.ascontiguousarray(v) for k, v in arrays.items()}
    args = {k[3:]: nc.dram_tensor(k, v.shape, _mybir.dt.from_np(v.dtype), kind="ExternalInput").ap()
            for k, v in arrays.items()}
    out = nc.dram_tensor("out_0", (IMAGES, SEQ, D), _mybir.dt.float32, kind="ExternalOutput").ap()
    early_fusion(nc, args, out)
    r = _run(nc, [arrays], core_ids=[0])
    return r.results[0]["out_0"]
```
